# Optimizing a Trainium2 kernel written in Bass

```python
import numpy as np
import jax
import jax.numpy as jnp

def _softmax(x, axis=-1):
    return jax.nn.softmax(x, axis=axis)

def _gelu(x):
    return jax.nn.gelu(x, approximate=True)

def _silu(x):
    return jax.nn.silu(x)

def _sigmoid(x):
    return jax.nn.sigmoid(x)

def _layernorm(x, axis=-1, eps=1e-05):
    m = jnp.mean(x, axis=axis, keepdims=True)
    v = jnp.var(x, axis=axis, keepdims=True)
    return (x - m) / jnp.sqrt(v + eps)

def _scatter_add(tgt, idx, src, axis=0):
    return tgt.at[idx].add(src)

def _segment_sum(src, seg, n):
    return jax.ops.segment_sum(src, seg, n)
kernel_name = 'mk_flamingo_gated_d1_seqx_r4_a6e964'

def setup_inputs(seed: int=0):
    np.random.seed(seed)
    _w = jnp.asarray

    def _rec_inputs():
        import jax
        import jax.numpy as jnp
        _rk = jax.random.key(seed)
        x = 7.22e-05 + 1 * jax.random.normal(jax.random.fold_in(_rk, 1), (4, 512, 512), jnp.float32)
        _lenS = 512 - jax.random.randint(jax.random.fold_in(_rk, 7), (4,), 0, max(1, 512 // 4) + 1, jnp.int32)
        _lenS2 = 512 - jax.random.randint(jax.random.fold_in(_rk, 8), (4,), 0, max(1, 512 // 4) + 1, jnp.int32)
        _ctx_1024P = jax.random.normal(jax.random.fold_in(_rk, 11), (4, 16, 256), jnp.float32)
        _ctx_1024c = jax.random.dirichlet(jax.random.fold_in(_rk, 511), 0.3 * jnp.ones((16,), jnp.float32), (4, 512))
        _ctx_1024t = jnp.einsum('bsk,bkd->bsd', _ctx_1024c, _ctx_1024P)
        _ctx_1024t = _ctx_1024t * jax.lax.rsqrt(jnp.mean(jnp.square(_ctx_1024t)) + 1e-12) * 0.953939
        ctx_1024 = 2.81802e-05 + 1.00001 * (_ctx_1024t + 0.3 * jax.random.normal(jax.random.fold_in(_rk, 611), (4, 512, 256), jnp.float32))
        _g = jax.random.normal(jax.random.fold_in(_rk, 9001), (2, 1), jnp.float32)
        _g = jnp.sign(_g) * jnp.maximum(jnp.abs(_g), 1.0) + (_g == 0) * 1.0
        g_xattn = _g[0]
        g_ffn = _g[1]
        return (x, ctx_1024, g_xattn, g_ffn)
    x, ctx_1024, g_xattn, g_ffn = _rec_inputs()

    def _L0_xattn_setup():
        import jax, jax.numpy as jnp
        import numpy as np
        key = jax.random.key(seed)
        ks = jax.random.split(key, 6)
        B, L, N, C, D = (8, 128, 512, 256, 128)
        return {'teacher_logits': jax.random.normal(ks[0], (B, L, N), dtype=jnp.float32), 'teacher_features': jax.random.normal(ks[1], (B, N, C), dtype=jnp.float32), 'Wq': jax.random.normal(ks[2], (D, C), dtype=jnp.float32) * (1.0 / np.sqrt(C)), 'bq': jnp.zeros((D,), dtype=jnp.float32), 'Wk': jax.random.normal(ks[3], (D, C), dtype=jnp.float32) * (1.0 / np.sqrt(C)), 'bk': jnp.zeros((D,), dtype=jnp.float32)}
    _L0_xattn_all = _L0_xattn_setup()
    _L0_xattn_in = {k: v for k, v in _L0_xattn_all.items() if k in ('Wq', 'bq', 'Wk', 'bk')}
    del _L0_xattn_all

    def _L0_ffn_setup():
        import jax, jax.numpy as jnp
        import numpy as np
        TOP_K = 6
        CAP_FACTOR = 2

        def _moe_block(x2d, wg_router, w_gate, w_up, w_down, ws_gate, ws_up, ws_down):
            T, D = x2d.shape
            E = wg_router.shape[0]
            scores = jax.nn.softmax(x2d @ wg_router.T, axis=-1)
            topk_w, topk_idx = jax.lax.top_k(scores, TOP_K)
            topk_w = topk_w / (jnp.sum(topk_w, axis=-1, keepdims=True) + 1e-20)
            flat_idx = topk_idx.reshape(-1)
            oh = jax.nn.one_hot(flat_idx, E, dtype=jnp.int32)
            pos = jnp.cumsum(oh, axis=0) - 1
            pos_in_e = jnp.take_along_axis(pos, flat_idx[:, None], axis=1)[:, 0]
            C = CAP_FACTOR * (T * TOP_K // E)
            valid = pos_in_e < C
            safe_pos = jnp.where(valid, pos_in_e, 0)
            tok_id = jnp.repeat(jnp.arange(T), TOP_K)
            vmask = valid[:, None].astype(x2d.dtype)
            x_rep = x2d[tok_id] * vmask
            xe = jnp.zeros((E, C, D), x2d.dtype).at[flat_idx, safe_pos].add(x_rep)
            g = jnp.einsum('ecd,edf->ecf', xe, w_gate)
            u = jnp.einsum('ecd,edf->ecf', xe, w_up)
            ye = jnp.einsum('ecf,efd->ecd', jax.nn.silu(g) * u, w_down)
            y_tok = ye[flat_idx, safe_pos] * vmask
            y = jnp.sum(y_tok.reshape(T, TOP_K, D) * topk_w[..., None], axis=1)
            sh = jax.nn.silu(x2d @ ws_gate) * (x2d @ ws_up) @ ws_down
            return y + sh
        key = jax.random.key(seed)
        ks = jax.random.split(key, 9)
        B, S, D, F, E = (1, 512, 512, 352, 32)
        FS = F * 2
        s = 0.02
        return {'hidden_states': jax.random.normal(ks[0], (B, S, D), jnp.float32), 'wg_router': jax.random.normal(ks[1], (E, D), jnp.float32) * s, 'w_gate': jax.random.normal(ks[2], (E, D, F), jnp.float32) * s, 'w_up': jax.random.normal(ks[3], (E, D, F), jnp.float32) * s, 'w_down': jax.random.normal(ks[4], (E, F, D), jnp.float32) * s, 'ws_gate': jax.random.normal(ks[5], (D, FS), jnp.float32) * s, 'ws_up': jax.random.normal(ks[6], (D, FS), jnp.float32) * s, 'ws_down': jax.random.normal(ks[7], (FS, D), jnp.float32) * s}
    _L0_ffn_all = _L0_ffn_setup()
    _L0_ffn_in = {k: v for k, v in _L0_ffn_all.items() if k in ('wg_router', 'w_gate', 'w_up', 'w_down', 'ws_gate', 'ws_up', 'ws_down')}
    del _L0_ffn_all
    return {'x': x, 'ctx_1024': ctx_1024, 'g_xattn': g_xattn, 'g_ffn': g_ffn, 'L0_xattn_Wq': _L0_xattn_in['Wq'], 'L0_xattn_bq': _L0_xattn_in['bq'], 'L0_xattn_Wk': _L0_xattn_in['Wk'], 'L0_xattn_bk': _L0_xattn_in['bk'], 'L0_ffn_wg_router': _L0_ffn_in['wg_router'], 'L0_ffn_w_gate': _L0_ffn_in['w_gate'], 'L0_ffn_w_up': _L0_ffn_in['w_up'], 'L0_ffn_w_down': _L0_ffn_in['w_down'], 'L0_ffn_ws_gate': _L0_ffn_in['ws_gate'], 'L0_ffn_ws_up': _L0_ffn_in['ws_up'], 'L0_ffn_ws_down': _L0_ffn_in['ws_down']}

def reference(x, ctx_1024, g_xattn, g_ffn, L0_xattn_Wq, L0_xattn_bq, L0_xattn_Wk, L0_xattn_bk, L0_ffn_wg_router, L0_ffn_w_gate, L0_ffn_w_up, L0_ffn_w_down, L0_ffn_ws_gate, L0_ffn_ws_up, L0_ffn_ws_down):
    import jax
    import jax.numpy as jnp

    def _L0_xattn_ref(teacher_logits, teacher_features, Wq, bq, Wk, bk):
        import jax, jax.numpy as jnp
        import numpy as np
        query = jnp.einsum('bnc,dc->bnd', teacher_features, Wq) + bq
        key = jnp.einsum('bnc,dc->bnd', teacher_features, Wk) + bk
        energy = jnp.einsum('bnd,bmd->bnm', query, key)
        attention = jax.nn.softmax(energy, axis=-1)
        x_m = jnp.einsum('bln,bmn->blm', teacher_logits, attention)
        return x_m

    def _L0_ffn_ref(hidden_states, wg_router, w_gate, w_up, w_down, ws_gate, ws_up, ws_down):
        import jax, jax.numpy as jnp
        import numpy as np
        TOP_K = 6
        CAP_FACTOR = 2

        def _moe_block(x2d, wg_router, w_gate, w_up, w_down, ws_gate, ws_up, ws_down):
            T, D = x2d.shape
            E = wg_router.shape[0]
            scores = jax.nn.softmax(x2d @ wg_router.T, axis=-1)
            topk_w, topk_idx = jax.lax.top_k(scores, TOP_K)
            topk_w = topk_w / (jnp.sum(topk_w, axis=-1, keepdims=True) + 1e-20)
            flat_idx = topk_idx.reshape(-1)
            oh = jax.nn.one_hot(flat_idx, E, dtype=jnp.int32)
            pos = jnp.cumsum(oh, axis=0) - 1
            pos_in_e = jnp.take_along_axis(pos, flat_idx[:, None], axis=1)[:, 0]
            C = CAP_FACTOR * (T * TOP_K // E)
            valid = pos_in_e < C
            safe_pos = jnp.where(valid, pos_in_e, 0)
            tok_id = jnp.repeat(jnp.arange(T), TOP_K)
            vmask = valid[:, None].astype(x2d.dtype)
            x_rep = x2d[tok_id] * vmask
            xe = jnp.zeros((E, C, D), x2d.dtype).at[flat_idx, safe_pos].add(x_rep)
            g = jnp.einsum('ecd,edf->ecf', xe, w_gate)
            u = jnp.einsum('ecd,edf->ecf', xe, w_up)
            ye = jnp.einsum('ecf,efd->ecd', jax.nn.silu(g) * u, w_down)
            y_tok = ye[flat_idx, safe_pos] * vmask
            y = jnp.sum(y_tok.reshape(T, TOP_K, D) * topk_w[..., None], axis=1)
            sh = jax.nn.silu(x2d @ ws_gate) * (x2d @ ws_up) @ ws_down
            return y + sh
        B, S, D = hidden_states.shape
        x2d = hidden_states.reshape(-1, D)
        out = _moe_block(x2d, wg_router, w_gate, w_up, w_down, ws_gate, ws_up, ws_down)
        return out.reshape(B, S, D)
    x = x + jnp.tanh(g_xattn[0]) * _L0_xattn_ref(_layernorm(x, axis=-1), ctx_1024, L0_xattn_Wq, L0_xattn_bq, L0_xattn_Wk, L0_xattn_bk)
    x = x + jnp.tanh(g_ffn[0]) * _L0_ffn_ref(_layernorm(x, axis=-1), L0_ffn_wg_router, L0_ffn_w_gate, L0_ffn_w_up, L0_ffn_w_down, L0_ffn_ws_gate, L0_ffn_ws_up, L0_ffn_ws_down)
    return x

_drawn_inputs = setup_inputs


def setup_inputs(seed=0):
    import zlib

    import numpy as np

    out = dict(_drawn_inputs(seed))
    spreads = {'L0_xattn_bq': (0.0, 0.1), 'L0_xattn_bk': (0.0, 0.8)}
    factors = {'L0_ffn_wg_router': 4.431,
     'L0_ffn_w_gate': 4.054,
     'L0_ffn_w_up': 3.958,
     'L0_ffn_w_down': 3.96}
    for name, (base, spread) in spreads.items():
        noise = np.random.default_rng([zlib.crc32(name.encode()), seed]).standard_normal(out[name].shape)
        drawn = base * np.exp(spread * noise) if base else spread * noise
        out[name] = jnp.asarray(drawn.astype(out[name].dtype))
    for name, factor in factors.items():
        out[name] = (out[name] * factor).astype(out[name].dtype)
    return out
```

```python
from contextlib import ExitStack

import concourse.bass as bass
from concourse import mybir

F32 = mybir.dt.float32
F32R = mybir.dt.float32r
BF16 = mybir.dt.bfloat16
I32 = mybir.dt.int32
ALU = mybir.AluOpType
ACT = mybir.ActivationFunctionType
AX = mybir.AxisListType.X

P = 128
EPS = 1e-5
TOPK = 6
GATE, UP, DOWN = range(3)


def gated_attention_moe(nc, x, ctx_in, g_xattn, g_ffn, Wq, bq, Wk, bk, wg_router, w_gate, w_up, w_down,
                        ws_gate, ws_up, ws_down, out):
    B, L, D = x.shape
    CX = ctx_in.shape[2]
    E, _, F = w_gate.shape
    T = B * L
    NT = T // P
    LT = L // P
    KD = D // P
    KC = CX // P
    KF = -(-F // P)
    FR = F - (KF - 1) * P
    HALVES = ws_gate.shape[1] // F
    CAP = 2 * (T * TOPK // E)
    NBLK = CAP // P
    MAIN = 4
    TRASH = T
    NV = 6
    SH = NT * HALVES
    assert HALVES == 2 and LT == 4 and KD == 4 and D == 512 and NBLK == 6 and SH == E and E % 2 == 0

    xn_dram = nc.dram_tensor("xn_rows", (T + P, D), F32, kind="Internal").ap()
    acc_dram = nc.dram_tensor("acc_rows", (T + P, D), F32, kind="Internal").ap()

    x_rows = x.rearrange("b l d -> (b l) d")
    ctx_rows = ctx_in.rearrange("b l d -> (b l) d")
    out_rows = out.rearrange("b l d -> (b l) d")

    with ExitStack() as stack:
        def sb(name, shape, dt=F32):
            return stack.enter_context(nc.sbuf_tensor(name, shape, dt))

        def sem(name):
            return stack.enter_context(nc.semaphore(name))

        bank = [stack.enter_context(nc.psum_tensor(f"bank{i}", [P, 512], F32)) for i in range(8)]

        x_sb = sb("x_sb", [P, NT, D])
        w_hi = [[sb(f"w_hi{s}_{p}", [P, KD if p < DOWN else KF, F if p < DOWN else D], F32R) for p in range(3)]
                for s in range(2)]
        w_lo = [[sb(f"w_lo{s}_{p}", [P, KD if p < DOWN else KF, F if p < DOWN else D], F32R) for p in range(3)]
                for s in range(2)]
        ident = sb("ident", [P, P])
        ones_bf = sb("ones_bf", [P, P], BF16)
        before = sb("before", [P, P], BF16)
        tanh_g = sb("tanh_g", [P, 2])
        g_raw = sb("g_raw", [P, 2])
        expd = sb("expd", [P, NT, E])
        top_f = sb("top_f", [P, NT, 8])
        denom = sb("denom", [P, NT])
        trash_row = sb("trash_row", [P, 1])
        neg_trash_row = sb("neg_trash_row", [P, 1])
        zeros = sb("zeros", [P, D])
        iota_e = sb("iota_e", [P, E])
        iota_a = sb("iota_a", [P, NBLK])
        iota_s = sb("iota_s", [P, P], BF16)
        fixed3 = sb("fixed3", [P, NT, 3], BF16)

        def stage_a_memory():
            inner = ExitStack()

            def sa(name, shape, dt=F32):
                return inner.enter_context(nc.sbuf_tensor(name, shape, dt))
            return inner, dict(
                ctx_sb=[sa(f"ctx_sb{i}", [P, LT, CX]) for i in range(2)],
                wqk=sa("wqk", [P, 2, CX]), b_qk=sa("b_qk", [P, 2]), rout=sa("rout", [E, D]),
                wqkT=[sa(f"wqkT{i}", [P, 2, KC, P], F32R) for i in range(2)],
                routT=[sa(f"routT{i}", [P, KD, E], F32R) for i in range(2)],
                ctxT=[sa(f"ctxT{i}", [P, KC, L], F32R) for i in range(2)],
                qkT=[sa(f"qkT{i}", [P, 2, L], F32R) for i in range(2)],
                xl=sa("xl", [P, LT, D]),
                xlT=[sa(f"xlT{i}", [P, LT, KD, P], F32R) for i in range(2)],
                prob=[sa(f"prob{i}", [P, L]) for i in range(2)],
                attT=[sa(f"attT{i}", [P, KD, L], F32R) for i in range(2)],
                xn=[sa(f"xn{i}", [P, D]) for i in range(2)],
                xnT=[[sa(f"xnT{i}_{s}", [P, KD, P], F32R) for s in range(2)] for i in range(2)],
                stats=sa("stats", [P, 2 * LT, 6]), mv=sa("mv", [P, 2 * LT, 2]), ve=sa("ve", [P, 2 * LT]),
                rstd=sa("rstd", [P, 2 * LT]), minus_half=sa("minus_half", [P, LT]),
                logit=sa("logit", [P, LT, E]), top8=sa("top8", [P, LT, 8]), neg_top=sa("neg_top", [P, LT]),
                top_at=sa("top_at", [P, LT, 8], mybir.dt.uint32),
                neg_max=sa("neg_max", [P, LT]), psum_row=sa("psum_row", [P, LT]), r_row=sa("r_row", [P, LT]),
            )

        def stage_b_memory():
            inner = ExitStack()

            def sa(name, shape, dt=F32):
                return inner.enter_context(nc.sbuf_tensor(name, shape, dt))
            return inner, dict(
                raw=[sa(f"raw{p}", [P, KD if p < DOWN else KF, F if p < DOWN else D]) for p in range(3)],
                xg=[sa(f"xg{i}", [P, D]) for i in range(2)],
                xT=[[sa(f"xT{i}_{s}", [P, KD, P], F32R) for s in range(2)] for i in range(2)],
                silu=sa("silu", [P, F]), h=sa("h", [P, F]),
                hT=[sa(f"hT{i}", [P, KF, P], F32R) for i in range(2)],
                ys=[sa(f"ys{i}", [P, D]) for i in range(2)],
                score=sa("score", [P, NT, E]), mask=sa("mask", [P, NT, E]), hit=sa("hit", [P, NT, E]),
                mask_bf=sa("mask_bf", [P, NT, E], BF16), rank=sa("rank", [P, NT, E]),
                rank_i=sa("rank_i", [P, NT, E], I32), blk_i=sa("blk_i", [P, NT, E], I32),
                blk=sa("blk", [P, NT, E]), pos=sa("pos", [P, NT, E], BF16),
                tsum=sa("tsum", [P, NT]), trec=sa("trec", [P, NT]),
                rz=sa("rz", [P, NT]),
                w3=sa("w3", [P, NT, E, 3], BF16), most=sa("most", [P, 1]), most_i=sa("most_i", [P, 1], I32),
                onehot=[sa(f"onehot{i}", [P, NT, P], BF16) for i in range(2)],
                in_blk=sa("in_blk", [P, NT, NBLK], BF16),
                vals=[sa(f"vals{i}", [P, NT, NV, NBLK], BF16) for i in range(2)],
                tab=sa("tab", [P, 4, NV, NBLK]), t1=sa("t1", [P, 4, NBLK]), t2=sa("t2", [P, 4, NBLK]),
                u1=sa("u1", [P, 4, NBLK]), u2=sa("u2", [P, 4, NBLK]),
                row_tab=sa("row_tab", [P, E * NBLK], I32), w_tab=sa("w_tab", [P, E * NBLK]),
                idx=[sa(f"idx{i}", [P, 1], I32) for i in range(2 * MAIN)],
            )

        inner_a, A = stage_a_memory()
        inner_a.close()
        inner_b, S = stage_b_memory()
        inner_b.close()

        consts_done = sem("consts_done")
        iota_done = sem("iota_done")
        small_loaded = sem("small_loaded")
        x_in = [sem(f"x_in{b}") for b in range(B)]
        ctx_in_sem = [sem(f"ctx_in{i}") for i in range(2)]
        tanh_done = sem("tanh_done")
        tp_psum = sem("tp_psum")
        tp_hi = sem("tp_hi")
        tp_lo = sem("tp_lo")
        qk_psum = sem("qk_psum")
        qk_hi = sem("qk_hi")
        qk_lo = sem("qk_lo")
        stat_link = sem("stat_link")
        stats_done = sem("stats_done")
        rstd_link = sem("rstd_link")
        rstd_done = sem("rstd_done")
        xl_done = sem("xl_done")
        energy_done = sem("energy_done")
        max_done = sem("max_done")
        exp_done = sem("exp_done")
        norm_link = sem("norm_link")
        prob_done = sem("prob_done")
        attend_done = sem("attend_done")
        x2_done = sem("x2_done")
        xn_done = sem("xn_done")
        xn_stored = [sem(f"xn_stored{i}") for i in range(2)]
        logit_psum = sem("logit_psum")
        logit_done = sem("logit_done")
        top_link = sem("top_link")
        index_done = sem("index_done")
        top_kept = sem("top_kept")
        top_done = sem("top_done")
        rexp_done = sem("rexp_done")
        route = sem("route")
        mask_ready = sem("mask_ready")
        ranked = sem("ranked")
        most_ready = sem("most_ready")
        raw_in = [sem(f"raw_in{p}") for p in range(3)]
        w_hi_done = sem("w_hi_done")
        w_ready = sem("w_ready")
        xg_in = [sem(f"xg_in{i}") for i in range(2)]
        xT_psum = sem("xT_psum")
        xT_hi = sem("xT_hi")
        xT_lo = sem("xT_lo")
        gu_done = sem("gu_done")
        silu_done = sem("silu_done")
        h_done = sem("h_done")
        hT_psum = sem("hT_psum")
        hT_hi = sem("hT_hi")
        hT_lo = sem("hT_lo")
        down_done = sem("down_done")
        shared_added = sem("shared_added")
        y_scaled = sem("y_scaled")
        acc_written = sem("acc_written")
        added = [sem(f"added{i}") for i in range(2)]
        in_blk_done = sem("in_blk_done")
        vals_done = sem("vals_done")
        tab_psum = sem("tab_psum")
        tab_link = sem("tab_link")
        tab_copied = sem("tab_copied")
        tab_done = sem("tab_done")
        idx_done = sem("idx_done")
        out_done = sem("out_done")
        o_w_in = sem("o_w_in")
        o_idx = sem("o_idx")
        o_x_in = sem("o_x_in")
        o_x_psum = sem("o_x_psum")
        o_xT = sem("o_xT")
        o_gu = sem("o_gu")
        o_silu = sem("o_silu")
        o_h = sem("o_h")
        o_h_psum = sem("o_h_psum")
        o_hT = sem("o_hT")
        o_down = sem("o_down")
        o_scaled = sem("o_scaled")
        o_added = sem("o_added")
        REST = NBLK - MAIN

        UNITS = KC + LT + LT + LT
        U_CTX, U_X, U_ATT, U_XN = 0, KC, KC + LT, KC + 2 * LT

        def unit(b, k):
            return 2 + b * UNITS + k

        def shared_piece(n, p):
            f0 = n * F
            if p == DOWN:
                return ws_down[f0:f0 + F, :]
            return (ws_gate, ws_up)[p][:, f0:f0 + F]

        def expert_piece(e, p):
            return (w_gate, w_up, w_down)[p][bass.ds(e, 1), :, :].rearrange("a d f -> (a d) f")


        def main_added(eng):
            eng.wait_ge(added[0], 16 * (E * MAIN // 2))
            eng.wait_ge(added[1], 16 * (E * MAIN // 2))

        def most_rows(eng):
            eng.wait_ge(most_ready, 1)
            return eng.value_load(S["most_i"][0:1, 0:1], min_val=0, max_val=T)

        o_x, o_y = S["xg"][0], S["ys"][0]
        o_xT_sb = S["ys"][1][:].rearrange("p (c t) -> p c t", t=P)
        o_hT_sb = S["xg"][1][:, 0:KF * P].rearrange("p (c t) -> p c t", t=P)

        block = stack.enter_context(nc.Block())

        @block.sync
        def _(sp):
            def load_ctx(b, par):
                sp.dma_start(A["ctx_sb"][par][:], ctx_rows[bass.ds(b * L, L), :].rearrange("(t p) c -> p t c", p=P)
                             ).then_inc(ctx_in_sem[par], 16)

            def load_x(b):
                sp.dma_start(x_sb[:, b * LT:(b + 1) * LT, :],
                             x_rows[b * L:(b + 1) * L, :].rearrange("(t p) d -> p t d", p=P)).then_inc(x_in[b], 16)

            def load_raw(src, p, n):
                if isinstance(n, int) and n == 0:
                    pass
                else:
                    sp.wait_ge(w_ready, 3 * n - 2 + p)
                if p < DOWN:
                    sp.dma_start(S["raw"][p][:], src.rearrange("(c p) f -> p c f", p=P)).then_inc(raw_in[p], 16)
                else:
                    sp.dma_start(S["raw"][p][:, 0:KF - 1, :],
                                 src[0:(KF - 1) * P, :].rearrange("(c p) d -> p c d", p=P)).then_inc(raw_in[p], 16)
                    sp.dma_start(S["raw"][p][0:FR, KF - 1, :], src[(KF - 1) * P:F, :]).then_inc(raw_in[p], 16)

            sp.dma_start(A["wqk"][:, 0, :], Wq).then_inc(small_loaded, 16)
            sp.dma_start(A["wqk"][:, 1, :], Wk).then_inc(small_loaded, 16)
            load_ctx(0, 0)
            load_x(0)
            sp.dma_start(A["b_qk"][:, 0:1], bq.rearrange("(d a) -> d a", a=1)).then_inc(small_loaded, 16)
            sp.dma_start(A["b_qk"][:, 1:2], bk.rearrange("(d a) -> d a", a=1)).then_inc(small_loaded, 16)
            sp.dma_start(A["rout"][:], wg_router).then_inc(small_loaded, 16)
            sp.dma_start(g_raw[:, 0:1], g_xattn.partition_broadcast(P)).then_inc(small_loaded, 16)
            sp.dma_start(g_raw[:, 1:2], g_ffn.partition_broadcast(P)).then_inc(small_loaded, 16)
            load_ctx(1, 1)
            for b in range(1, B):
                load_x(b)
            sp.wait_ge(consts_done, 1)
            sp.dma_start(xn_dram[T:T + P, :], zeros[:]).then_inc(xn_stored[0], 16)
            sp.dma_start(acc_dram[T:T + P, :], zeros[:]).then_inc(xn_stored[1], 16)

            with sp.Fori(0, B // 2) as i:
                for par in range(2):
                    b = 2 * i + par
                    for lt in range(LT):
                        sp.wait_ge(xn_done, b * LT + lt + 1)
                        sp.dma_start(xn_dram[bass.ds((b * LT + lt) * P, P), :], A["xn"][lt % 2][:]
                                     ).then_inc(xn_stored[lt % 2], 16)
                    sp.wait_ge(tp_psum, unit(b, U_CTX + KC))
                    load_ctx(par + 2, par)

            sp.wait_ge(tp_psum, unit(B, 0))
            sp.wait_ge(tp_lo, unit(B, 0))
            sp.wait_ge(logit_psum, NT)
            for q in range(2):
                sp.wait_ge(xn_stored[q], 16 * (1 + NT // 2))
                sp.wait_ge(ctx_in_sem[q], 16 * (1 + B // 2))
            for n in range(2):
                for p in range(3):
                    load_raw(shared_piece(n, p), p, n)
            for p in range(3):
                load_raw(expert_piece(0, p), p, 2)
            with sp.Fori(0, NT) as t:
                sp.wait_ge(shared_added, t + 1)
                sp.dma_start(acc_dram[bass.ds(t * P, P), :],
                             x_sb[:, bass.ds(t, 1), :].rearrange("p a d -> p (a d)")).then_inc(acc_written, 16)
            with sp.Fori(1, E) as e:
                for p in range(3):
                    load_raw(expert_piece(e, p), p, e + 2)
            main_added(sp)
            with sp.If(most_rows(sp) > MAIN * P):
                def load_whole(e):
                    for p in range(2):
                        sp.dma_start(S["raw"][p][:], expert_piece(e, p).rearrange("(c p) f -> p c f", p=P)
                                     ).then_inc(o_w_in, 16)
                    src = expert_piece(e, DOWN)
                    sp.dma_start(S["raw"][DOWN][:, 0:KF - 1, :],
                                 src[0:(KF - 1) * P, :].rearrange("(c p) d -> p c d", p=P)).then_inc(o_w_in, 16)
                    sp.dma_start(S["raw"][DOWN][0:FR, KF - 1, :], src[(KF - 1) * P:F, :]).then_inc(o_w_in, 16)

                load_whole(0)
                with sp.Fori(1, E) as e:
                    sp.wait_ge(o_down, REST * e)
                    load_whole(e)
                sp.wait_ge(o_added, 16 * REST * E)
            sp.dma_start(out_rows, acc_dram[0:T, :]).then_inc(out_done, 16)
            sp.wait_ge(out_done, 16)

        @block.gpsimd
        def _(pool):
            pool.memset(zeros[:], 0.0).then_inc(consts_done, 1)
            pool.memset(ident[:], 0.0).then_inc(consts_done, 1)
            pool.memset(ones_bf[:], 1.0).then_inc(consts_done, 1)
            pool.memset(A["minus_half"][:], -0.5).then_inc(consts_done, 1)
            pool.wait_ge(consts_done, 4)
            pool.affine_select(out=ident[:], in_=ident[:], compare_op=ALU.not_equal, fill=1.0, base=0,
                               pattern=[[-1, P]], channel_multiplier=1).then_inc(consts_done, 1)
            pool.affine_select(out=before[:], in_=ones_bf[:], compare_op=ALU.is_gt, fill=0.0, base=0,
                               pattern=[[1, P]], channel_multiplier=-1).then_inc(iota_done, 1)
            pool.iota(iota_e[:], [[1, E]], base=0, channel_multiplier=0,
                      allow_small_or_imprecise_dtypes=True).then_inc(iota_done, 1)
            pool.iota(iota_a[:], [[1, NBLK]], base=0, channel_multiplier=0,
                      allow_small_or_imprecise_dtypes=True).then_inc(iota_done, 1)
            pool.iota(iota_s[:], [[1, P]], base=0, channel_multiplier=0,
                      allow_small_or_imprecise_dtypes=True).then_inc(iota_done, 1)
            pool.iota(fixed3[:, :, 1], [[1, NT]], base=0, channel_multiplier=0,
                      allow_small_or_imprecise_dtypes=True).then_inc(iota_done, 1)
            pool.iota(fixed3[:, :, 2], [[0, NT]], base=0, channel_multiplier=1,
                      allow_small_or_imprecise_dtypes=True).then_inc(iota_done, 1)
            pool.memset(fixed3[:, :, 0], 1.0).then_inc(iota_done, 1)
            pool.iota(trash_row[:], [[0, 1]], base=TRASH, channel_multiplier=1,
                      allow_small_or_imprecise_dtypes=True).then_inc(iota_done, 1)
            pool.iota(neg_trash_row[:], [[0, 1]], base=-TRASH, channel_multiplier=-1,
                      allow_small_or_imprecise_dtypes=True).then_inc(iota_done, 1)

            def inv_std(k, lo, n):
                pool.wait_ge(stats_done, k + 1)
                pool.nop(nofuse=True)
                pool.tensor_scalar(A["ve"][:, lo:lo + n], A["mv"][:, lo:lo + n, 1], EPS, None, ALU.add
                                   ).then_inc(rstd_link, 1)
                pool.wait_ge(rstd_link, k + 1)
                pool.tensor_tensor(A["rstd"][:, lo:lo + n], A["ve"][:, lo:lo + n], A["minus_half"][:, 0:n],
                                   ALU.pow).then_inc(rstd_done, 1)

            with pool.Fori(0, B) as b:
                k = b * (1 + LT)
                inv_std(k, 0, LT)
                for lt in range(LT):
                    inv_std(k + 1 + lt, LT + lt, 1)

            def free_xg(X):
                pool.wait_ge(xT_psum, X - 1)

            def load_xg(X, par):
                pool.dma_start(S["xg"][par][:], xn_dram[bass.ds(X * P, P), :]).then_inc(xg_in[par], 16)

            pool.wait_ge(tp_psum, unit(B, 0))
            pool.wait_ge(tp_lo, unit(B, 0))
            for q in range(2):
                pool.wait_ge(xn_stored[q], 16 * (1 + NT // 2))
                pool.wait_ge(ctx_in_sem[q], 16 * (1 + B // 2))
            pool.wait_ge(logit_psum, NT)
            load_xg(0, 0)
            load_xg(1, 1)
            with pool.Fori(1, NT // 2) as i:
                for par in range(2):
                    free_xg(2 * i + par)
                    load_xg(2 * i + par, par)

            def index(r, k, e, j):
                pool.tensor_copy(S["idx"][k][:], S["row_tab"][:, bass.ds(e * NBLK + j, 1)]).then_inc(idx_done, 1)

            def gather(r, k):
                pool.wait_ge(idx_done, r + 1)
                free_xg(NT + r)
                pool.nop(nofuse=True)
                pool.indirect_dma_start(out=S["xg"][k % 2][:], out_offset=None, in_=xn_dram,
                                        in_offset=bass.IndirectOffsetOnAxis(ap=S["idx"][k][:], axis=0)
                                        ).then_inc(xg_in[k % 2], 16)

            pool.wait_ge(tab_done, 1)
            for k in range(2):
                index(k, k, 0, k)
                gather(k, k)
            pool.wait_ge(tab_done, E // 4)

            def pool_pair(i, first, last):
                r0 = 2 * MAIN * i
                for k in range(2 * MAIN):
                    r = r0 + k
                    if not (last and k >= 2 * MAIN - 2):
                        kk = (k + 2) % (2 * MAIN)
                        e2 = 2 * i + (k + 2) // MAIN
                        index(r + 2, kk, e2, (k + 2) % MAIN)
                        gather(r + 2, kk)
                    if not (first and k == 0):
                        scatter_at(i, k - 1, first)
                if last:
                    scatter_at(i, 2 * MAIN - 1, first)

            def scatter_at(i, k, first):
                if k < 0:
                    i, k = i - 1, 2 * MAIN - 1
                r0 = 2 * MAIN * i
                pool.wait_ge(y_scaled, r0 + k + 1)
                if first and k == 0:
                    pool.wait_ge(acc_written, 16 * NT)
                else:
                    pool.wait_ge(added[(k + 1) % 2], 16 * (MAIN * i) + 16 * ((k + 1) // 2))
                pool.nop(nofuse=True)
                pool.indirect_dma_start(out=acc_dram, in_=S["ys"][k % 2][:], in_offset=None,
                                        out_offset=bass.IndirectOffsetOnAxis(ap=S["idx"][k][:], axis=0),
                                        compute_op=ALU.add).then_inc(added[k % 2], 16)

            pool_pair(0, True, False)
            with pool.Fori(1, E // 2 - 1) as i:
                pool_pair(i, False, False)
            pool_pair(E // 2 - 1, False, True)

            main_added(pool)
            with pool.If(most_rows(pool) > MAIN * P):
                with pool.Fori(0, E) as e:
                    for j in range(REST):
                        q = REST * e + j
                        pool.tensor_copy(S["idx"][0][:], S["row_tab"][:, bass.ds(e * NBLK + MAIN + j, 1)]
                                         ).then_inc(o_idx, 1)
                        pool.wait_ge(o_idx, q + 1)
                        pool.nop(nofuse=True)
                        pool.indirect_dma_start(out=o_x[:], out_offset=None, in_=xn_dram,
                                                in_offset=bass.IndirectOffsetOnAxis(ap=S["idx"][0][:], axis=0)
                                                ).then_inc(o_x_in, 16)
                        pool.wait_ge(o_scaled, q + 1)
                        pool.nop(nofuse=True)
                        pool.indirect_dma_start(out=acc_dram, in_=o_y[:], in_offset=None,
                                                out_offset=bass.IndirectOffsetOnAxis(ap=S["idx"][0][:], axis=0),
                                                compute_op=ALU.add).then_inc(o_added, 16)
                        pool.wait_ge(o_added, 16 * (q + 1))

        @block.scalar
        def _(act):
            act.wait_ge(small_loaded, 16 * 7)
            act.activation(tanh_g[:], g_raw[:], ACT.Tanh).then_inc(tanh_done, 1)

            def round_unit(u, par, dst, cols=512, shape=None):
                act.wait_ge(tp_psum, u + 1)
                src = bank[par][:, 0:cols]
                act.activation(dst, src if shape is None else shape(src), ACT.Copy).then_inc(tp_hi, 1)

            chunks = lambda v: v.rearrange("p (c t) -> p c t", t=P)
            round_unit(0, 0, A["wqkT"][0][:].rearrange("p a c d -> p (a c) d"), shape=chunks)
            round_unit(1, 1, A["routT"][0][:], KD * E, lambda v: v.rearrange("p (c e) -> p c e", e=E))

            with act.Fori(0, B) as b:
                def u(k):
                    return unit(b, k), k % 2
                for c in range(KC):
                    round_unit(*u(U_CTX + c), A["ctxT"][0][:, c, :])
                for j in range(2):
                    act.wait_ge(qk_psum, 2 * b + j + 1)
                    act.activation(A["qkT"][0][:, j, :], bank[2 + j][:], ACT.Identity, bias=A["b_qk"][:, j:j + 1]
                                   ).then_inc(qk_hi, 1)
                for lt in range(LT):
                    round_unit(*u(U_X + lt), A["xlT"][0][:, lt, :, :], shape=chunks)

                def soft(mt):
                    act.wait_ge(max_done, b * LT + mt + 1)
                    if mt >= 2:
                        act.wait_ge(tp_psum, unit(b, U_ATT + mt - 2) + 1)
                    act.activation(A["prob"][mt % 2][:], bank[4 + mt % 2][:], ACT.Exp,
                                   bias=A["neg_max"][:, mt:mt + 1], accum_out=A["psum_row"][:, mt:mt + 1]
                                   ).then_inc(exp_done, 1)
                soft(0)
                soft(1)
                for mt in range(LT):
                    round_unit(*u(U_ATT + mt), A["attT"][0][:, :, mt * P:(mt + 1) * P], shape=chunks)
                    if mt + 2 < LT:
                        soft(mt + 2)

                def keep_logit(lt):
                    act.wait_ge(logit_psum, b * LT + lt + 1)
                    act.activation(A["logit"][:, lt, :], bank[2 + lt % 2][:, 0:E], ACT.Copy).then_inc(logit_done, 1)
                for lt in range(LT):
                    round_unit(*u(U_XN + lt), A["xnT"][0][lt % 2][:], shape=chunks)
                    if lt:
                        keep_logit(lt - 1)
                keep_logit(LT - 1)
                for lt in range(LT):
                    tile = b * LT + lt
                    act.wait_ge(top_done, tile + 1)
                    act.activation(expd[:, bass.ds(tile, 1), :].rearrange("p a e -> p (a e)"),
                                   A["logit"][:, lt, :], ACT.Exp,
                                   bias=A["neg_top"][:, lt:lt + 1], accum_out=denom[:, bass.ds(tile, 1)]
                                   ).then_inc(rexp_done, 1)

            def weight_hi(n, slot, p, after_gu=None, after_down=None):
                act.wait_ge(raw_in[p], 16 * (n + 1) if p < DOWN else 32 * (n + 1))
                if p < DOWN and after_gu is not None:
                    act.wait_ge(gu_done, after_gu)
                if p == DOWN and after_down is not None:
                    act.wait_ge(down_done, after_down)
                if p < DOWN:
                    act.activation(w_hi[slot][p][:], S["raw"][p][:], ACT.Copy).then_inc(w_hi_done, 1)
                else:
                    act.activation(w_hi[slot][p][:, 0:KF - 1, :], S["raw"][p][:, 0:KF - 1, :], ACT.Copy
                                   ).then_inc(w_hi_done, 1)
                    act.activation(w_hi[slot][p][0:FR, KF - 1, :], S["raw"][p][0:FR, KF - 1, :], ACT.Copy
                                   ).then_inc(w_hi_done, 1)

            def do_silu(g):
                act.wait_ge(gu_done, g + 1)
                if not (isinstance(g, int) and g == 0):
                    act.wait_ge(h_done, g)
                act.activation(S["silu"][:], bank[1][:, 0:F], ACT.Silu).then_inc(silu_done, 1)

            def xT_hi_part(X, par):
                act.wait_ge(xT_psum, X + 1)
                act.activation(S["xT"][0][par][:], chunks(bank[0][:]), ACT.Copy).then_inc(xT_hi, 1)

            def hT_hi_part(g):
                act.wait_ge(hT_psum, g + 1)
                src = chunks(bank[3][:, 0:KF * P])
                act.activation(S["hT"][0][:, 0:KF - 1, :], src[:, 0:KF - 1, :], ACT.Copy).then_inc(hT_hi, 1)
                act.activation(S["hT"][0][0:FR, KF - 1, :], src[0:FR, KF - 1, :], ACT.Copy).then_inc(hT_hi, 1)

            def scale_y(i, k):
                if k < 0:
                    i, k = i - 1, 2 * MAIN - 1
                r = 2 * MAIN * i + k
                act.wait_ge(down_done, SH + r + 1)
                if not (isinstance(i, int) and i == 0 and k < 2):
                    act.wait_ge(added[k % 2], 16 * MAIN * i + 16 * (k // 2))
                act.activation(S["ys"][k % 2][:], bank[4][:], ACT.Copy,
                               scale=S["w_tab"][:, bass.ds((2 * i + k // MAIN) * NBLK + k % MAIN, 1)]
                               ).then_inc(y_scaled, 1)

            act.wait_ge(tp_psum, unit(B, 0))
            act.wait_ge(tp_lo, unit(B, 0))
            act.wait_ge(logit_psum, NT)
            for n in range(2):
                for p in range(3):
                    weight_hi(n, n, p)
            for X in range(1):
                xT_hi_part(0, 0)

            def act_shared(i, last):
                for j in range(4):
                    g = 4 * i + j
                    do_silu(g)
                    if j % 2 == 1:
                        xT_hi_part(2 * i + j // 2 + 1, (j // 2 + 1) % 2)
                    if last and j == 3:
                        for p in range(2):
                            weight_hi(2, 0, p, after_gu=SH - 1)
                    hT_hi_part(g)
                    if last and j == 3:
                        weight_hi(2, 0, DOWN, after_down=SH - 1)

            act_shared(0, False)
            with act.Fori(1, SH // 4 - 1) as i:
                act_shared(i, False)
            act_shared(SH // 4 - 1, True)

            act.wait_ge(tab_done, E // 4)

            def act_pair(i, first, last):
                for k in range(2 * MAIN):
                    r = 2 * MAIN * i + k
                    do_silu(SH + r)
                    if not (last and k == 2 * MAIN - 1):
                        xT_hi_part(NT + r + 1, (k + 1) % 2)
                    if not (first and k == 0):
                        scale_y(i, k - 1)
                    hT_hi_part(SH + r)
                    j = k % MAIN
                    e = 2 * i + k // MAIN
                    if j >= 1 and not (last and k >= MAIN):
                        weight_hi(e + 3, (k // MAIN + 1) % 2, j - 1, after_gu=SH + MAIN * e, after_down=SH + MAIN * e)
                if last:
                    scale_y(i, 2 * MAIN - 1)

            act_pair(0, True, False)
            with act.Fori(1, E // 2 - 1) as i:
                act_pair(i, False, False)
            act_pair(E // 2 - 1, False, True)

            main_added(act)
            with act.If(most_rows(act) > MAIN * P):
                with act.Fori(0, E) as e:
                    for j in range(REST):
                        q = REST * e + j
                        act.wait_ge(o_x_psum, q + 1)
                        act.activation(o_xT_sb, chunks(bank[0][:]), ACT.Copy).then_inc(o_xT, 1)
                        act.wait_ge(o_gu, q + 1)
                        act.activation(S["silu"][:], bank[1][:, 0:F], ACT.Silu).then_inc(o_silu, 1)
                        act.wait_ge(o_h_psum, q + 1)
                        src = chunks(bank[3][:, 0:KF * P])
                        act.activation(o_hT_sb[:, 0:KF - 1, :], src[:, 0:KF - 1, :], ACT.Copy).then_inc(o_hT, 1)
                        act.activation(o_hT_sb[0:FR, KF - 1, :], src[0:FR, KF - 1, :], ACT.Copy).then_inc(o_hT, 1)
                        act.wait_ge(o_down, q + 1)
                        act.activation(o_y[:], bank[4][:], ACT.Copy,
                                       scale=S["w_tab"][:, bass.ds(e * NBLK + MAIN + j, 1)]).then_inc(o_scaled, 1)
                act.wait_ge(o_scaled, REST * E)

        @block.vector
        def _(dve):
            chunks = lambda v: v.rearrange("p (c t) -> p c t", t=P)

            def rest_unit(u, par, hi, lo, cols=512, shape=None):
                dve.wait_ge(tp_hi, u + 1)
                src = bank[par][:, 0:cols]
                dve.tensor_tensor(lo, src if shape is None else shape(src), hi, ALU.subtract).then_inc(tp_lo, 1)

            rest_unit(0, 0, A["wqkT"][0][:].rearrange("p a c d -> p (a c) d"),
                      A["wqkT"][1][:].rearrange("p a c d -> p (a c) d"), shape=chunks)
            rest_unit(1, 1, A["routT"][0][:], A["routT"][1][:], KD * E, lambda v: v.rearrange("p (c e) -> p c e", e=E))

            STATS = LT + LT
            for q in range(B):
                dve.wait_ge(x_in[q], 16)
            dve.wait_ge(tanh_done, 1)
            with dve.Fori(0, B) as b:
                for lt in range(LT):
                    dve.bn_stats(A["stats"][:, lt, :], x_sb[:, bass.ds(b * LT + lt, 1), :].rearrange("p a d -> p (a d)")
                                 ).then_inc(stat_link, 1)
                dve.wait_ge(stat_link, b * STATS + LT)
                dve.nop(nofuse=True)
                for lt in range(LT):
                    ins = dve.bn_aggr(A["mv"][:, lt, :], A["stats"][:, lt, :])
                ins.then_inc(stats_done, 1)
                for c in range(KC):
                    rest_unit(unit(b, U_CTX + c), c % 2, A["ctxT"][0][:, c, :], A["ctxT"][1][:, c, :])
                for j in range(2):
                    dve.wait_ge(qk_hi, 2 * b + j + 1)
                    dve.scalar_tensor_tensor(A["qkT"][1][:, j, :], bank[2 + j][:], A["b_qk"][:, j:j + 1],
                                             A["qkT"][0][:, j, :].bitcast(F32), ALU.add, ALU.subtract).then_inc(qk_lo, 1)
                dve.wait_ge(rstd_done, b * (1 + LT) + 1)
                for lt in range(LT):
                    dve.tensor_scalar(A["xl"][:, lt, :], x_sb[:, bass.ds(b * LT + lt, 1), :].rearrange("p a d -> p (a d)"),
                                      A["mv"][:, lt, 0:1], A["rstd"][:, lt:lt + 1], ALU.subtract, ALU.mult
                                      ).then_inc(xl_done, 1)
                for lt in range(LT):
                    rest_unit(unit(b, U_X + lt), lt % 2, A["xlT"][0][:, lt, :, :], A["xlT"][1][:, lt, :, :], shape=chunks)

                def row_max(mt):
                    dve.wait_ge(energy_done, b * LT + mt + 1)
                    dve.tensor_reduce(A["neg_max"][:, mt:mt + 1], bank[4 + mt % 2][:], AX, ALU.max, negate=True
                                      ).then_inc(max_done, 1)
                row_max(0)
                row_max(1)
                for mt in range(LT):
                    dve.wait_ge(exp_done, b * LT + mt + 1)
                    dve.reciprocal(A["r_row"][:, mt:mt + 1], A["psum_row"][:, mt:mt + 1]).then_inc(norm_link, 1)
                    dve.wait_ge(norm_link, b * LT + mt + 1)
                    dve.tensor_scalar(A["prob"][mt % 2][:], A["prob"][mt % 2][:], A["r_row"][:, mt:mt + 1], None,
                                      ALU.mult).then_inc(prob_done, 1)
                    rest_unit(unit(b, U_ATT + mt), mt % 2, A["attT"][0][:, :, mt * P:(mt + 1) * P],
                              A["attT"][1][:, :, mt * P:(mt + 1) * P], shape=chunks)
                    if mt + 2 < LT:
                        row_max(mt + 2)

                def best(lt):
                    dve.wait_ge(logit_done, b * LT + lt + 1)
                    dve.nop(nofuse=True)
                    dve.max(A["top8"][:, lt, :], A["logit"][:, lt, :]).then_inc(top_link, 1)
                    dve.wait_ge(top_link, b * LT + lt + 1)
                    dve.nop(nofuse=True)
                    dve.max_index(A["top_at"][:, lt, :], A["top8"][:, lt, :], A["logit"][:, lt, :]
                                  ).then_inc(index_done, 1)
                    dve.tensor_scalar(A["neg_top"][:, lt:lt + 1], A["top8"][:, lt, 0:1], -1.0, None, ALU.mult
                                      ).then_inc(top_done, 1)

                def rest_xn(lt):
                    rest_unit(unit(b, U_XN + lt), lt % 2, A["xnT"][0][lt % 2][:], A["xnT"][1][lt % 2][:], shape=chunks)

                for lt in range(LT):
                    tile = b * LT + lt
                    row = x_sb[:, bass.ds(tile, 1), :].rearrange("p a d -> p (a d)")
                    dve.wait_ge(attend_done, tile + 1)
                    dve.scalar_tensor_tensor(row, bank[6 + lt % 2][:], tanh_g[:, 0:1], row, ALU.mult, ALU.add
                                             ).then_inc(x2_done, 1)
                    dve.wait_ge(x2_done, tile + 1)
                    dve.nop(nofuse=True)
                    dve.bn_stats(A["stats"][:, LT + lt, :], row).then_inc(stat_link, 1)
                    dve.wait_ge(stat_link, b * STATS + LT + lt + 1)
                    dve.nop(nofuse=True)
                    dve.bn_aggr(A["mv"][:, LT + lt, :], A["stats"][:, LT + lt, :]).then_inc(stats_done, 1)
                    if lt:
                        rest_xn(lt - 1)
                    if lt >= 2:
                        best(lt - 2)
                    dve.wait_ge(rstd_done, b * (1 + LT) + 2 + lt)
                    if lt >= 2:
                        dve.wait_ge(tp_psum, unit(b, U_XN + lt - 2) + 1)
                    dve.wait_ge(xn_stored[lt % 2], 16 * (1 + (LT // 2) * b + lt // 2))
                    dve.tensor_scalar(A["xn"][lt % 2][:], row, A["mv"][:, LT + lt, 0:1], A["rstd"][:, LT + lt:LT + lt + 1],
                                      ALU.subtract, ALU.mult).then_inc(xn_done, 1)
                rest_xn(LT - 1)
                best(LT - 2)
                best(LT - 1)
                dve.wait_ge(index_done, (b + 1) * LT)
                dve.tensor_copy(top_f[:, bass.ds(b * LT, LT), :], A["top_at"][:]).then_inc(top_kept, 1)

            step = [0]

            def link(ins):
                step[0] += 1
                ins.then_inc(route, 1)
                dve.wait_ge(route, step[0])

            dve.wait_ge(rexp_done, NT)
            dve.wait_ge(logit_psum, NT)
            for q in range(2):
                dve.wait_ge(xn_stored[q], 16 * (1 + NT // 2))
                dve.wait_ge(ctx_in_sem[q], 16 * (1 + B // 2))
            dve.wait_ge(iota_done, 9)
            over_e = lambda v: v[:].rearrange("p (t a) -> p t a", a=1).to_broadcast([P, NT, E])
            dve.wait_ge(top_kept, B)
            iota_all = iota_e[:].rearrange("p (a e) -> p a e", a=1).to_broadcast([P, NT, E])
            for k in range(TOPK):
                at_k = top_f[:, :, k:k + 1].to_broadcast([P, NT, E])
                link(dve.tensor_tensor(S["mask" if k == 0 else "hit"][:], iota_all, at_k, ALU.is_equal))
                if k:
                    link(dve.tensor_tensor(S["mask"][:], S["mask"][:], S["hit"][:], ALU.add))
            dve.tensor_copy(S["mask_bf"][:], S["mask"][:]).then_inc(mask_ready, 1)
            link(dve.reciprocal(S["rz"][:], denom[:]))
            link(dve.tensor_tensor(S["score"][:], expd[:], over_e(S["rz"]), ALU.mult))
            link(dve.tensor_tensor(S["score"][:], S["score"][:], S["mask"][:], ALU.mult))
            link(dve.tensor_reduce(S["tsum"][:], S["score"][:], AX, ALU.add))
            link(dve.tensor_scalar(S["tsum"][:], S["tsum"][:], 1e-20, None, ALU.add))
            link(dve.reciprocal(S["trec"][:], S["tsum"][:]))
            link(dve.tensor_tensor(S["score"][:], S["score"][:], over_e(S["trec"]), ALU.mult))
            for part in range(3):
                link(dve.tensor_copy(S["w3"][:, :, :, part], S["score"][:]))
                if part < 2:
                    link(dve.tensor_tensor(S["score"][:], S["score"][:], S["w3"][:, :, :, part], ALU.subtract))
            dve.wait_ge(ranked, 1)
            ranks = bank[6][:].rearrange("p (t e) -> p t e", e=E)
            link(dve.scalar_tensor_tensor(S["rank"][:], S["mask"][:], float(-4 * T), ranks, ALU.mult, ALU.add))
            link(dve.tensor_scalar(S["rank_i"][:], S["rank"][:], float(4 * T), None, ALU.add))
            link(dve.tensor_scalar(S["blk_i"][:], S["rank_i"][:], 7, None, ALU.arith_shift_right))
            link(dve.tensor_scalar(S["rank_i"][:], S["rank_i"][:], P - 1, None, ALU.bitwise_and))
            link(dve.tensor_copy(S["blk"][:], S["blk_i"][:]))
            link(dve.tensor_copy(S["pos"][:], S["rank_i"][:]))
            link(dve.tensor_reduce(S["most"][:], bank[7][:, 0:E], AX, ALU.max))
            dve.tensor_copy(S["most_i"][:], S["most"][:]).then_inc(most_ready, 1)

            def weight_lo(n, slot, p):
                if p < DOWN:
                    dve.wait_ge(w_hi_done, 4 * n + p + 1)
                    dve.tensor_tensor(w_lo[slot][p][:], S["raw"][p][:], w_hi[slot][p][:], ALU.subtract
                                      ).then_inc(w_ready, 1)
                else:
                    dve.wait_ge(w_hi_done, 4 * n + 4)
                    dve.tensor_tensor(w_lo[slot][p][:, 0:KF - 1, :], S["raw"][p][:, 0:KF - 1, :],
                                      w_hi[slot][p][:, 0:KF - 1, :], ALU.subtract)
                    dve.tensor_tensor(w_lo[slot][p][0:FR, KF - 1, :], S["raw"][p][0:FR, KF - 1, :],
                                      w_hi[slot][p][0:FR, KF - 1, :], ALU.subtract).then_inc(w_ready, 1)

            def make_h(g):
                dve.wait_ge(silu_done, g + 1)
                if not (isinstance(g, int) and g == 0):
                    dve.wait_ge(hT_psum, g)
                dve.tensor_tensor(S["h"][:], bank[2][:, 0:F], S["silu"][:], ALU.mult).then_inc(h_done, 1)

            def xT_lo_part(X, par):
                dve.wait_ge(xT_hi, X + 1)
                dve.tensor_tensor(S["xT"][1][par][:], chunks(bank[0][:]), S["xT"][0][par][:], ALU.subtract
                                  ).then_inc(xT_lo, 1)

            def hT_lo_part(g):
                dve.wait_ge(hT_hi, 2 * g + 2)
                src = chunks(bank[3][:, 0:KF * P])
                dve.tensor_tensor(S["hT"][1][:, 0:KF - 1, :], src[:, 0:KF - 1, :], S["hT"][0][:, 0:KF - 1, :],
                                  ALU.subtract)
                dve.tensor_tensor(S["hT"][1][0:FR, KF - 1, :], src[0:FR, KF - 1, :], S["hT"][0][0:FR, KF - 1, :],
                                  ALU.subtract).then_inc(hT_lo, 1)

            def add_shared(t):
                dve.wait_ge(down_done, 2 * t + 2)
                row = x_sb[:, bass.ds(t, 1), :].rearrange("p a d -> p (a d)")
                dve.scalar_tensor_tensor(row, bank[4][:], tanh_g[:, 1:2], row, ALU.mult, ALU.add
                                         ).then_inc(shared_added, 1)

            def table_values(e, par, first):
                if not first:
                    dve.wait_ge(tab_psum, e - 1)
                blk_e = S["blk"][:, :, bass.ds(e, 1)].to_broadcast([P, NT, NBLK])
                a_all = iota_a[:].rearrange("p (o a) -> p o a", o=1).to_broadcast([P, NT, NBLK])
                dve.tensor_tensor(S["in_blk"][:], a_all, blk_e, ALU.is_equal).then_inc(in_blk_done, 1)
                pos_e = S["pos"][:, :, bass.ds(e, 1)].to_broadcast([P, NT, P])
                s_all = iota_s[:].rearrange("p (a s) -> p a s", a=1).to_broadcast([P, NT, P])
                dve.tensor_tensor(S["onehot"][par][:], s_all, pos_e, ALU.is_equal)
                dve.wait_ge(in_blk_done, e + 1)
                in4 = S["in_blk"][:].rearrange("p t (o a) -> p t o a", o=1).to_broadcast([P, NT, 3, NBLK])
                f4 = fixed3[:].rearrange("p t (v o) -> p t v o", o=1).to_broadcast([P, NT, 3, NBLK])
                w4 = S["w3"][:, :, bass.ds(e, 1), :].rearrange("p t o v -> p t v o").to_broadcast([P, NT, 3, NBLK])
                dve.tensor_tensor(S["vals"][par][:, :, 0:3, :], in4, f4, ALU.mult)
                dve.tensor_tensor(S["vals"][par][:, :, 3:6, :], in4, w4, ALU.mult).then_inc(vals_done, 1)

            def finish_tables(i):
                dve.wait_ge(tab_psum, 4 * i + 4)
                tab = S["tab"]
                dve.tensor_copy(tab[:].rearrange("p e v a -> p (e v a)"), bank[5][:, 0:4 * NV * NBLK]
                                ).then_inc(tab_copied, 1)
                dve.wait_ge(tab_copied, i + 1)
                dve.scalar_tensor_tensor(S["t1"][:], tab[:, :, 1, :], float(P), tab[:, :, 2, :], ALU.mult, ALU.add
                                         ).then_inc(tab_link, 1)
                dve.tensor_tensor(S["u1"][:], tab[:, :, 3, :], tab[:, :, 4, :], ALU.add).then_inc(tab_link, 1)
                dve.wait_ge(tab_link, 4 * i + 1)
                dve.scalar_tensor_tensor(S["t2"][:], tab[:, :, 0, :], neg_trash_row[:, 0:1], S["t1"][:], ALU.mult,
                                         ALU.add).then_inc(tab_link, 1)
                dve.wait_ge(tab_link, 4 * i + 2)
                dve.tensor_tensor(S["u2"][:], S["u1"][:], tab[:, :, 5, :], ALU.add).then_inc(tab_link, 1)
                dve.wait_ge(tab_link, 4 * i + 3)
                flat = lambda v: v[:].rearrange("p e a -> p (e a)")
                dve.tensor_scalar(S["row_tab"][:, bass.ds(4 * NBLK * i, 4 * NBLK)], flat(S["t2"]), trash_row[:, 0:1],
                                  None, ALU.add)
                dve.wait_ge(tab_link, 4 * i + 4)
                dve.tensor_scalar(S["w_tab"][:, bass.ds(4 * NBLK * i, 4 * NBLK)], flat(S["u2"]), tanh_g[:, 1:2],
                                  None, ALU.mult).then_inc(tab_done, 1)

            for n in range(2):
                for p in range(3):
                    weight_lo(n, n, p)
            xT_lo_part(0, 0)

            def dve_shared(i, first, last):
                for j in range(4):
                    g = 4 * i + j
                    make_h(g)
                    if j % 2 == 1:
                        xT_lo_part(2 * i + j // 2 + 1, (j // 2 + 1) % 2)
                    elif not (first and j == 0):
                        add_shared(2 * i + j // 2 - 1)
                    if last and j == 3:
                        for p in range(2):
                            weight_lo(2, 0, p)
                    hT_lo_part(g)
                    if last and j == 3:
                        weight_lo(2, 0, DOWN)
                    table_values(g, j % 2, first and j < 2)
                finish_tables(i)

            dve_shared(0, True, False)
            with dve.Fori(1, SH // 4 - 1) as i:
                dve_shared(i, False, False)
            dve_shared(SH // 4 - 1, False, True)

            def dve_pair(i, first, last):
                for k in range(2 * MAIN):
                    r = 2 * MAIN * i + k
                    make_h(SH + r)
                    if first and k == 0:
                        add_shared(NT - 1)
                    if not (last and k == 2 * MAIN - 1):
                        xT_lo_part(NT + r + 1, (k + 1) % 2)
                    hT_lo_part(SH + r)
                    j = k % MAIN
                    e = 2 * i + k // MAIN
                    if j >= 1 and not (last and k >= MAIN):
                        weight_lo(e + 3, (k // MAIN + 1) % 2, j - 1)

            dve_pair(0, True, False)
            with dve.Fori(1, E // 2 - 1) as i:
                dve_pair(i, False, False)
            dve_pair(E // 2 - 1, False, True)

            main_added(dve)
            with dve.If(most_rows(dve) > MAIN * P):
                with dve.Fori(0, REST * E) as q:
                    dve.wait_ge(o_silu, q + 1)
                    dve.tensor_tensor(S["h"][:], bank[2][:, 0:F], S["silu"][:], ALU.mult).then_inc(o_h, 1)
                dve.wait_ge(o_h, REST * E)

        @block.tensor
        def _(pe):
            def product(ps, lhs, rhs, start, stop):
                pe.matmul(ps, lhs[0], rhs[0], start=start, stop=False)
                pe.matmul(ps, lhs[0], rhs[1], start=False, stop=False)
                return pe.matmul(ps, lhs[1], rhs[0], start=False, stop=stop)

            def unit_free(u):
                pe.wait_ge(tp_lo, u - 1)

            pe.wait_ge(consts_done, 5)
            pe.wait_ge(small_loaded, 16 * 7)
            for a in range(2):
                for c in range(KC):
                    ins = pe.transpose(bank[0][:, (a * KC + c) * P:(a * KC + c + 1) * P],
                                       A["wqk"][:, a, c * P:(c + 1) * P], ident[:])
            ins.then_inc(tp_psum, 1)
            for c in range(KD):
                ins = pe.transpose(bank[1][:, c * E:(c + 1) * E], A["rout"][:, c * P:(c + 1) * P], ident[0:E, 0:E])
            ins.then_inc(tp_psum, 1)

            def batch(b, par):
                ctx_sb = A["ctx_sb"][par]
                pe.wait_ge(ctx_in_sem[par], 16 * ((b - par) // 2 + 1) if isinstance(b, int) else 16 * ctx_round(b))
                for c in range(KC):
                    unit_free(unit(b, U_CTX + c))
                    for t in range(LT):
                        ins = pe.transpose(bank[c % 2][:, t * P:(t + 1) * P], ctx_sb[:, t, c * P:(c + 1) * P], ident[:])
                    ins.then_inc(tp_psum, 1)
                pe.wait_ge(tp_lo, unit(b, U_CTX + KC))
                for a in range(2):
                    for c in range(KC):
                        ins = product(bank[2 + a][:], [A["wqkT"][s][:, a, c, :] for s in range(2)],
                                      [A["ctxT"][s][:, c, :] for s in range(2)], c == 0, c == KC - 1)
                    ins.then_inc(qk_psum, 1)
                for lt in range(LT):
                    unit_free(unit(b, U_X + lt))
                    pe.wait_ge(xl_done, b * LT + lt + 1)
                    for c in range(KD):
                        ins = pe.transpose(bank[lt % 2][:, c * P:(c + 1) * P], A["xl"][:, lt, c * P:(c + 1) * P], ident[:])
                    ins.then_inc(tp_psum, 1)

                def energy(mt):
                    if mt >= 2:
                        pe.wait_ge(exp_done, b * LT + mt - 1)
                    product(bank[4 + mt % 2][:], [A["qkT"][s][:, 0, mt * P:(mt + 1) * P] for s in range(2)],
                            [A["qkT"][s][:, 1, :] for s in range(2)], True, True).then_inc(energy_done, 1)

                pe.wait_ge(qk_lo, 2 * b + 2)
                energy(0)
                energy(1)
                for mt in range(LT):
                    unit_free(unit(b, U_ATT + mt))
                    pe.wait_ge(prob_done, b * LT + mt + 1)
                    for c in range(KD):
                        ins = pe.transpose(bank[mt % 2][:, c * P:(c + 1) * P], A["prob"][mt % 2][:, c * P:(c + 1) * P], ident[:])
                    ins.then_inc(tp_psum, 1)
                    if mt + 2 < LT:
                        energy(mt + 2)

                def attend(lt):
                    if lt >= 2:
                        pe.wait_ge(x2_done, b * LT + lt - 1)
                    for c in range(KD):
                        ins = product(bank[6 + lt % 2][:], [A["xlT"][s][:, lt, c, :] for s in range(2)],
                                      [A["attT"][s][:, c, :] for s in range(2)], c == 0, c == KD - 1)
                    ins.then_inc(attend_done, 1)

                def turn_xn(lt):
                    unit_free(unit(b, U_XN + lt))
                    pe.wait_ge(xn_done, b * LT + lt + 1)
                    for c in range(KD):
                        ins = pe.transpose(bank[lt % 2][:, c * P:(c + 1) * P], A["xn"][lt % 2][:, c * P:(c + 1) * P], ident[:])
                    ins.then_inc(tp_psum, 1)

                def logits(lt):
                    pe.wait_ge(tp_lo, unit(b, U_XN + lt) + 1)
                    if lt >= 2:
                        pe.wait_ge(logit_done, b * LT + lt - 1)
                    for c in range(KD):
                        ins = product(bank[2 + lt % 2][:, 0:E], [A["xnT"][s][lt % 2][:, c, :] for s in range(2)],
                                      [A["routT"][s][:, c, :] for s in range(2)], c == 0, c == KD - 1)
                    ins.then_inc(logit_psum, 1)

                pe.wait_ge(tp_lo, unit(b, U_ATT + LT))
                attend(0)
                attend(1)
                turn_xn(0)
                attend(2)
                turn_xn(1)
                logits(0)
                attend(3)
                turn_xn(2)
                logits(1)
                turn_xn(3)
                logits(2)
                logits(3)

            with pe.Fori(0, B // 2) as i:
                def ctx_round(b):
                    return i + 1
                for par in range(2):
                    batch(2 * i + par, par)

            pe.wait_ge(mask_ready, 1)
            pe.wait_ge(x2_done, NT)
            flat = S["mask_bf"][:].rearrange("p t e -> p (t e)")
            pe.matmul(bank[6][:], before[:], flat, start=True, stop=True)
            for d in range(1, NT):
                pe.matmul(bank[6][:, d * E:], ones_bf[:], flat[:, 0:(NT - d) * E], start=False, stop=True,
                          skip_group_check=True)
            for t in range(NT):
                ins = pe.matmul(bank[7][:, 0:E], ones_bf[:], flat[:, t * E:(t + 1) * E], start=t == 0, stop=t == NT - 1)
            ins.then_inc(ranked, 1)

            def turn_x(X, par, count):
                pe.wait_ge(xg_in[par], 16 * count)
                if not (isinstance(X, int) and X == 0):
                    pe.wait_ge(xT_lo, X)
                for c in range(KD):
                    ins = pe.transpose(bank[0][:, c * P:(c + 1) * P], S["xg"][par][:, c * P:(c + 1) * P], ident[:])
                ins.then_inc(xT_psum, 1)

            def gate_up(n, slot, X, par):
                pe.wait_ge(xT_lo, X + 1)
                pe.wait_ge(w_ready, 3 * n + 2)
                for c in range(KD):
                    for s, parts in ((0, (w_hi, w_lo)), (1, (w_hi,))):
                        for w in parts:
                            for q in range(2):
                                first = c == 0 and s == 0 and w is w_hi
                                ins = pe.matmul(bank[1 + q][:, 0:F], S["xT"][s][par][:, c, :], w[slot][q][:, c, :],
                                                start=first, stop=c == KD - 1 and s == 1)
                ins.then_inc(gu_done, 1)

            def turn_h(g):
                pe.wait_ge(h_done, g + 1)
                if not (isinstance(g, int) and g == 0):
                    pe.wait_ge(hT_lo, g)
                for c in range(KF):
                    n = P if c < KF - 1 else FR
                    ins = pe.transpose(bank[3][0:n, c * P:(c + 1) * P], S["h"][:, c * P:c * P + n], ident[:])
                ins.then_inc(hT_psum, 1)

            def down(g, n, slot, start, stop):
                pe.wait_ge(hT_lo, g + 1)
                pe.wait_ge(w_ready, 3 * n + 3)
                for c in range(KF):
                    k = P if c < KF - 1 else FR
                    ins = product(bank[4][:], [S["hT"][s][0:k, c, :] for s in range(2)],
                                  [w[slot][DOWN][0:k, c, :] for w in (w_hi, w_lo)],
                                  start and c == 0, stop and c == KF - 1)
                ins.then_inc(down_done, 1)

            def fill_table(e, j, first):
                pe.wait_ge(vals_done, e + 1)
                if j == 0 and not first:
                    pe.wait_ge(tab_copied, (e - j) // 4 if isinstance(e, int) else tabs(e))
                W = NV * NBLK
                for t in range(NT):
                    ins = pe.matmul(bank[5][:, j * W:(j + 1) * W], S["onehot"][j % 2][:, t, :],
                                    S["vals"][j % 2][:, t, :, :].rearrange("p v a -> p (v a)"),
                                    start=t == 0, stop=t == NT - 1)
                ins.then_inc(tab_psum, 1)

            def pe_shared(i, first):
                nonlocal_i[0] = i
                for j in range(4):
                    g = 4 * i + j
                    half, t = j % 2, 2 * i + j // 2
                    gate_up(half, half, t, (j // 2) % 2)
                    if half:
                        par = (j // 2 + 1) % 2
                        turn_x(t + 1, par, i + 1 + (j // 2 + 1) // 2)
                        if not (first and j == 1):
                            pe.wait_ge(shared_added, t)
                        down(g - 1, 0, 0, True, False)
                    elif not (first and j == 0):
                        down(g - 1, 1, 1, False, True)
                    turn_h(g)
                    fill_table(g, j, first)

            nonlocal_i = [0]

            def tabs(e):
                return nonlocal_i[0]

            turn_x(0, 0, 1)
            pe_shared(0, True)
            with pe.Fori(1, SH // 4) as i:
                pe_shared(i, False)

            def pe_pair(i, first, last):
                for k in range(2 * MAIN):
                    r = 2 * MAIN * i + k
                    e, j = 2 * i + k // MAIN, k % MAIN
                    slot = (k // MAIN) % 2
                    gate_up(2 + e, slot, NT + r, k % 2)
                    if not (last and k == 2 * MAIN - 1):
                        turn_x(NT + r + 1, (k + 1) % 2, NT // 2 + MAIN * i + 1 + (k + 1) // 2)
                    if first and k == 0:
                        down(SH - 1, 1, 1, False, True)
                    else:
                        if first and k == 1:
                            pe.wait_ge(shared_added, NT)
                        elif k >= 1:
                            pe.wait_ge(y_scaled, r - 1)
                        else:
                            pe.wait_ge(y_scaled, r - 1)
                        down(SH + r - 1, 2 + e - (1 if j == 0 else 0), slot if j else 1 - slot, True, True)
                    turn_h(SH + r)
                if last:
                    r = 2 * MAIN * (i + 1)
                    pe.wait_ge(y_scaled, r - 1)
                    down(SH + r - 1, 2 + E - 1, 1, True, True)

            pe_pair(0, True, False)
            with pe.Fori(1, E // 2 - 1) as i:
                pe_pair(i, False, False)
            pe_pair(E // 2 - 1, False, True)

            main_added(pe)
            with pe.If(most_rows(pe) > MAIN * P):
                with pe.Fori(0, E) as e:
                    for j in range(REST):
                        q = REST * e + j
                        pe.wait_ge(o_x_in, 16 * (q + 1))
                        for c in range(KD):
                            ins = pe.transpose(bank[0][:, c * P:(c + 1) * P], o_x[:, c * P:(c + 1) * P], ident[:])
                        ins.then_inc(o_x_psum, 1)
                        pe.wait_ge(o_xT, q + 1)
                        pe.wait_ge(o_w_in, 64 * (e + 1))
                        for p in range(2):
                            for c in range(KD):
                                ins = pe.matmul(bank[1 + p][:, 0:F], o_xT_sb[:, c, :], S["raw"][p][:, c, :],
                                                start=c == 0, stop=c == KD - 1)
                        ins.then_inc(o_gu, 1)
                        pe.wait_ge(o_h, q + 1)
                        for c in range(KF):
                            n = P if c < KF - 1 else FR
                            ins = pe.transpose(bank[3][0:n, c * P:(c + 1) * P], S["h"][:, c * P:c * P + n], ident[:])
                        ins.then_inc(o_h_psum, 1)
                        pe.wait_ge(o_hT, 2 * q + 2)
                        for c in range(KF):
                            n = P if c < KF - 1 else FR
                            ins = pe.matmul(bank[4][:], o_hT_sb[0:n, c, :], S["raw"][DOWN][0:n, c, :],
                                            start=c == 0, stop=c == KF - 1)
                        ins.then_inc(o_down, 1)
                pe.wait_ge(o_down, REST * E)


_INS = ['x', 'ctx_1024', 'g_xattn', 'g_ffn', 'L0_xattn_Wq', 'L0_xattn_bq', 'L0_xattn_Wk', 'L0_xattn_bk',
        'L0_ffn_wg_router', 'L0_ffn_w_gate', 'L0_ffn_w_up', 'L0_ffn_w_down', 'L0_ffn_ws_gate', 'L0_ffn_ws_up',
        'L0_ffn_ws_down']
_OUT = ((4, 512, 512), 'float32')


def kernel(**inputs):
    import numpy as _np
    import concourse.bacc as _bacc
    from concourse import mybir as _mybir
    from concourse.bass_utils import run_bass_kernel_spmd as _run

    nc = _bacc.Bacc("TRN2", target_bir_lowering=False, num_devices=1)
    arrays, args = {}, []
    for name in _INS:
        a = _np.ascontiguousarray(inputs[name])
        arrays[f"in_{name}"] = a
        args.append(nc.dram_tensor(f"in_{name}", a.shape, _mybir.dt.from_np(a.dtype), kind="ExternalInput").ap())
    shape, dtype = _OUT
    out = nc.dram_tensor("out_0", shape, _mybir.dt.from_np(_np.dtype(dtype)), kind="ExternalOutput").ap()
    gated_attention_moe(nc, *args, out)
    r = _run(nc, [arrays], core_ids=[0])
    return r.results[0]["out_0"]
```

```python
from contextlib import ExitStack

import concourse.bass as bass
from concourse import mybir

F32 = mybir.dt.float32
F32R = mybir.dt.float32r
BF16 = mybir.dt.bfloat16
I32 = mybir.dt.int32
ALU = mybir.AluOpType
ACT = mybir.ActivationFunctionType
AX = mybir.AxisListType.X

P = 128
EPS = 1e-5
TOPK = 6
GATE, UP, DOWN = range(3)


def gated_attention_moe(nc, x, ctx_in, g_xattn, g_ffn, Wq, bq, Wk, bk, wg_router, w_gate, w_up, w_down,
                        ws_gate, ws_up, ws_down, out):
    B, L, D = x.shape
    CX = ctx_in.shape[2]
    E, _, F = w_gate.shape
    T = B * L
    NT = T // P
    LT = L // P
    KD = D // P
    KC = CX // P
    KF = -(-F // P)
    FR = F - (KF - 1) * P
    HALVES = ws_gate.shape[1] // F
    CAP = 2 * (T * TOPK // E)
    NBLK = CAP // P
    MAIN = 4
    TRASH = T
    NV = 6
    SH = NT * HALVES
    assert HALVES == 2 and LT == 4 and KD == 4 and D == 512 and NBLK == 6 and SH == E and E % 2 == 0

    xn_dram = nc.dram_tensor("xn_rows", (T + P, D), F32, kind="Internal").ap()
    acc_dram = nc.dram_tensor("acc_rows", (T + P, D), F32, kind="Internal").ap()

    x_rows = x.rearrange("b l d -> (b l) d")
    ctx_rows = ctx_in.rearrange("b l d -> (b l) d")
    out_rows = out.rearrange("b l d -> (b l) d")

    with ExitStack() as stack:
        def sb(name, shape, dt=F32):
            return stack.enter_context(nc.sbuf_tensor(name, shape, dt))

        def sem(name):
            return stack.enter_context(nc.semaphore(name))

        bank = [stack.enter_context(nc.psum_tensor(f"bank{i}", [P, 512], F32)) for i in range(8)]

        x_sb = sb("x_sb", [P, NT, D])
        w_hi = [[sb(f"w_hi{s}_{p}", [P, KD if p < DOWN else KF, F if p < DOWN else D], F32R) for p in range(3)]
                for s in range(2)]
        w_lo = [[sb(f"w_lo{s}_{p}", [P, KD if p < DOWN else KF, F if p < DOWN else D], F32R) for p in range(3)]
                for s in range(2)]
        raw = [sb(f"raw{p}", [P, KD if p < DOWN else KF, F if p < DOWN else D]) for p in range(3)]
        ident = sb("ident", [P, P])
        ones_bf = sb("ones_bf", [P, P], BF16)
        before = sb("before", [P, P], BF16)
        tanh_g = sb("tanh_g", [P, 2])
        g_raw = sb("g_raw", [P, 2])
        expd = sb("expd", [P, NT, E])
        top_f = sb("top_f", [P, NT, 8])
        denom = sb("denom", [P, NT])
        trash_row = sb("trash_row", [P, 1])
        neg_trash_row = sb("neg_trash_row", [P, 1])
        iota_e = sb("iota_e", [P, E])
        iota_a = sb("iota_a", [P, NBLK])
        iota_s = sb("iota_s", [P, P], BF16)
        fixed3 = sb("fixed3", [P, NT, 3], BF16)

        def stage_a_memory():
            inner = ExitStack()

            def sa(name, shape, dt=F32):
                return inner.enter_context(nc.sbuf_tensor(name, shape, dt))
            return inner, dict(
                ctx_sb=sa("ctx_sb", [P, LT, CX]),
                b_qk=sa("b_qk", [P, 2]),
                wqkT=[sa(f"wqkT{i}", [P, 2, KC, P], F32R) for i in range(2)],
                routT=[sa(f"routT{i}", [P, KD, E], F32R) for i in range(2)],
                ctxT=[sa(f"ctxT{i}", [P, KC, L], F32R) for i in range(2)],
                qkT=[sa(f"qkT{i}", [P, 2, L], F32R) for i in range(2)],
                xl=sa("xl", [P, LT, D]),
                xlT=[sa(f"xlT{i}", [P, LT, KD, P], F32R) for i in range(2)],
                prob=[sa(f"prob{i}", [P, L]) for i in range(2)],
                attT=[sa(f"attT{i}", [P, KD, L], F32R) for i in range(2)],
                xn=[sa(f"xn{i}", [P, D]) for i in range(2)],
                xnT=[[sa(f"xnT{i}_{s}", [P, KD, P], F32R) for s in range(2)] for i in range(2)],
                stats=sa("stats", [P, 2 * LT, 6]), mv=sa("mv", [P, 2 * LT, 2]), ve=sa("ve", [P, 2 * LT]),
                rstd=sa("rstd", [P, 2 * LT]), neg_mean=sa("neg_mean", [P, 2 * LT]),
                shift=sa("shift", [P, 2 * LT]), minus_half=sa("minus_half", [P, LT]),
                logit=sa("logit", [P, LT, E]), top8=sa("top8", [P, LT, 8]), neg_top=sa("neg_top", [P, LT]),
                top_at=sa("top_at", [P, LT, 8], mybir.dt.uint32),
                neg_max=sa("neg_max", [P, LT]), psum_row=sa("psum_row", [P, LT]), r_row=sa("r_row", [P, LT]),
            )

        def stage_b_memory():
            inner = ExitStack()

            def sa(name, shape, dt=F32):
                return inner.enter_context(nc.sbuf_tensor(name, shape, dt))
            return inner, dict(
                xg=[sa(f"xg{i}", [P, D]) for i in range(2)],
                xT=[[sa(f"xT{i}_{s}", [P, KD, P], F32R) for s in range(2)] for i in range(2)],
                silu=sa("silu", [P, F]), h=sa("h", [P, F]),
                hT=[sa(f"hT{i}", [P, KF, P], F32R) for i in range(2)],
                ys=[sa(f"ys{i}", [P, D]) for i in range(2)],
                score=sa("score", [P, NT, E]), mask=sa("mask", [P, NT, E]), hit=sa("hit", [P, NT, E]),
                mask_bf=sa("mask_bf", [P, NT, E], BF16), rank=sa("rank", [P, NT, E]),
                rank_i=sa("rank_i", [P, NT, E], I32), blk_i=sa("blk_i", [P, NT, E], I32),
                blk=sa("blk", [P, NT, E]), pos=sa("pos", [P, NT, E], BF16),
                tsum=sa("tsum", [P, NT]), trec=sa("trec", [P, NT]),
                rz=sa("rz", [P, NT]),
                w3=sa("w3", [P, NT, E, 3], BF16), most=sa("most", [P, 1]), most_i=sa("most_i", [P, 1], I32),
                onehot=[sa(f"onehot{i}", [P, NT, P], BF16) for i in range(2)],
                in_blk=sa("in_blk", [P, NT, NBLK], BF16),
                vals=[sa(f"vals{i}", [P, NT, NV, NBLK], BF16) for i in range(2)],
                tab=sa("tab", [P, 4, NV, NBLK]), t1=sa("t1", [P, 4, NBLK]), t2=sa("t2", [P, 4, NBLK]),
                u1=sa("u1", [P, 4, NBLK]), u2=sa("u2", [P, 4, NBLK]),
                row_tab=sa("row_tab", [P, E * NBLK], I32), w_tab=sa("w_tab", [P, E * NBLK]),
                idx=[sa(f"idx{i}", [P, 1], I32) for i in range(2 * MAIN)],
            )

        inner_a, A = stage_a_memory()
        inner_a.close()
        A["wqk"] = A["prob"][0][:].rearrange("p (a c) -> p a c", a=2)
        A["rout"] = A["prob"][1][0:E, :]
        inner_b, S = stage_b_memory()
        inner_b.close()

        consts_done = sem("consts_done")
        iota_done = sem("iota_done")
        small_loaded = sem("small_loaded")
        x_in = [sem(f"x_in{b}") for b in range(B)]
        ctx_loaded = sem("ctx_loaded")
        tanh_done = sem("tanh_done")
        tp_psum = sem("tp_psum")
        tp_hi = sem("tp_hi")
        tp_lo = sem("tp_lo")
        qk_psum = sem("qk_psum")
        qk_hi = sem("qk_hi")
        qk_lo = sem("qk_lo")
        stat_link = sem("stat_link")
        stats_done = sem("stats_done")
        rstd_link = sem("rstd_link")
        rstd_done = sem("rstd_done")
        xl_done = sem("xl_done")
        energy_done = sem("energy_done")
        max_done = sem("max_done")
        exp_done = sem("exp_done")
        recip_done = sem("recip_done")
        prob_done = sem("prob_done")
        attend_done = sem("attend_done")
        x2_done = sem("x2_done")
        xn_done = sem("xn_done")
        xn_stored = [sem(f"xn_stored{i}") for i in range(2)]
        logit_psum = sem("logit_psum")
        logit_done = sem("logit_done")
        top_link = sem("top_link")
        index_done = sem("index_done")
        top_kept = sem("top_kept")
        top_done = sem("top_done")
        rexp_done = sem("rexp_done")
        route = sem("route")
        mask_ready = sem("mask_ready")
        ranked = sem("ranked")
        most_ready = sem("most_ready")
        raw_in = [sem(f"raw_in{p}") for p in range(3)]
        w_hi_done = sem("w_hi_done")
        w_ready = sem("w_ready")
        xg_in = [sem(f"xg_in{i}") for i in range(2)]
        xT_psum = sem("xT_psum")
        xT_hi = sem("xT_hi")
        xT_lo = sem("xT_lo")
        gu_done = sem("gu_done")
        silu_done = sem("silu_done")
        h_done = sem("h_done")
        hT_psum = sem("hT_psum")
        hT_hi = sem("hT_hi")
        hT_lo = sem("hT_lo")
        down_done = sem("down_done")
        shared_added = sem("shared_added")
        y_scaled = sem("y_scaled")
        acc_written = sem("acc_written")
        added = [sem(f"added{i}") for i in range(2)]
        in_blk_done = sem("in_blk_done")
        vals_done = sem("vals_done")
        tab_psum = sem("tab_psum")
        tab_link = sem("tab_link")
        tab_copied = sem("tab_copied")
        tab_done = sem("tab_done")
        idx_done = sem("idx_done")
        out_done = sem("out_done")
        o_w_in = sem("o_w_in")
        o_idx = sem("o_idx")
        o_x_in = sem("o_x_in")
        o_x_psum = sem("o_x_psum")
        o_xT = sem("o_xT")
        o_gu = sem("o_gu")
        o_silu = sem("o_silu")
        o_h = sem("o_h")
        o_h_psum = sem("o_h_psum")
        o_hT = sem("o_hT")
        o_down = sem("o_down")
        o_scaled = sem("o_scaled")
        o_added = sem("o_added")
        REST = NBLK - MAIN

        TURNS = ["ctx0", "ctx1", "xn0", "x0", "x1", "att0", "xn1", "att1", "x2", "xn2", "x3", "att2", "xn3", "att3"]
        BACK = [t for t in TURNS if t[:2] == "xn"]
        FRONT = [t for t in TURNS if t not in BACK]
        UNITS = 2 + len(FRONT) + (B - 1) * len(TURNS) + len(BACK)

        class Round:

            def __init__(self, f, b):
                self.f, self.b = f, b
                self.turns = TURNS if f is not None and b is not None else FRONT if b is None else BACK
                if b is None:
                    self.base = 2
                elif f is None:
                    self.base = UNITS - len(BACK)
                else:
                    self.base = 2 + len(FRONT) + b * len(TURNS)

            def unit(self, name):
                k = self.turns.index(name)
                return self.base + k, k % 2

        def shared_piece(n, p):
            f0 = n * F
            if p == DOWN:
                return ws_down[f0:f0 + F, :]
            return (ws_gate, ws_up)[p][:, f0:f0 + F]

        def expert_piece(e, p):
            return (w_gate, w_up, w_down)[p][bass.ds(e, 1), :, :].rearrange("a d f -> (a d) f")


        def main_added(eng):
            eng.wait_ge(added[0], 16 * (E * MAIN // 2))
            eng.wait_ge(added[1], 16 * (E * MAIN // 2))

        def most_rows(eng):
            eng.wait_ge(most_ready, 1)
            return eng.value_load(S["most_i"][0:1, 0:1], min_val=0, max_val=T)

        o_x, o_y = S["xg"][0], S["ys"][0]
        o_xT_sb = S["ys"][1][:].rearrange("p (c t) -> p c t", t=P)
        o_hT_sb = S["xg"][1][:, 0:KF * P].rearrange("p (c t) -> p c t", t=P)

        block = stack.enter_context(nc.Block())

        @block.sync
        def _(sp):
            def load_ctx(b):
                sp.dma_start(A["ctx_sb"][:], ctx_rows[bass.ds(b * L, L), :].rearrange("(t p) c -> p t c", p=P)
                             ).then_inc(ctx_loaded, 16)

            def load_x(b):
                sp.dma_start(x_sb[:, b * LT:(b + 1) * LT, :],
                             x_rows[b * L:(b + 1) * L, :].rearrange("(t p) d -> p t d", p=P)).then_inc(x_in[b], 16)

            def load_raw(src, p, n):
                if isinstance(n, int) and n == 0:
                    pass
                else:
                    sp.wait_ge(w_ready, 3 * n - 2 + p)
                if p < DOWN:
                    sp.dma_start(raw[p][:], src.rearrange("(c p) f -> p c f", p=P)).then_inc(raw_in[p], 16)
                else:
                    sp.dma_start(raw[p][:, 0:KF - 1, :],
                                 src[0:(KF - 1) * P, :].rearrange("(c p) d -> p c d", p=P)).then_inc(raw_in[p], 16)
                    sp.dma_start(raw[p][0:FR, KF - 1, :], src[(KF - 1) * P:F, :]).then_inc(raw_in[p], 16)

            sp.dma_start(A["wqk"][:, 0, :], Wq).then_inc(small_loaded, 16)
            sp.dma_start(A["wqk"][:, 1, :], Wk).then_inc(small_loaded, 16)
            load_ctx(0)
            load_x(0)
            sp.dma_start(A["b_qk"][:, 0:1], bq.rearrange("(d a) -> d a", a=1)).then_inc(small_loaded, 16)
            sp.dma_start(A["b_qk"][:, 1:2], bk.rearrange("(d a) -> d a", a=1)).then_inc(small_loaded, 16)
            sp.dma_start(A["rout"], wg_router).then_inc(small_loaded, 16)
            sp.dma_start(g_raw[:, 0:1], g_xattn.partition_broadcast(P)).then_inc(small_loaded, 16)
            sp.dma_start(g_raw[:, 1:2], g_ffn.partition_broadcast(P)).then_inc(small_loaded, 16)
            for p in range(3):
                load_raw(shared_piece(0, p), p, 0)
            for b in range(1, B):
                load_x(b)
            sp.wait_ge(consts_done, 2)
            sp.dma_start(xn_dram[T:T + P, :], A["xn"][0][:]).then_inc(xn_stored[0], 16)
            sp.dma_start(acc_dram[T:T + P, :], A["xn"][1][:]).then_inc(xn_stored[1], 16)
            first = Round(0, None)
            sp.wait_ge(tp_psum, first.unit("ctx1")[0] + 1)
            load_ctx(1)
            for p in range(3):
                load_raw(shared_piece(1, p), p, 1)

            def store_xn(b):
                for lt in range(LT):
                    sp.wait_ge(xn_done, b * LT + lt + 1)
                    sp.dma_start(xn_dram[bass.ds((b * LT + lt) * P, P), :], A["xn"][lt % 2][:]
                                 ).then_inc(xn_stored[lt % 2], 16)

            def store_and_load(b, more):
                if more:
                    sp.wait_ge(tp_psum, Round(b + 1, b).unit("ctx1")[0] + 1)
                    load_ctx(b + 2)
                store_xn(b)

            with sp.Fori(0, B - 2) as b:
                store_and_load(b, True)
            store_xn(B - 2)
            store_xn(B - 1)
            for p in range(3):
                load_raw(expert_piece(0, p), p, 2)
            with sp.Fori(0, NT) as t:
                sp.wait_ge(shared_added, t + 1)
                sp.dma_start(acc_dram[bass.ds(t * P, P), :],
                             x_sb[:, bass.ds(t, 1), :].rearrange("p a d -> p (a d)")).then_inc(acc_written, 16)
            with sp.Fori(1, E) as e:
                for p in range(3):
                    load_raw(expert_piece(e, p), p, e + 2)
            main_added(sp)
            with sp.If(most_rows(sp) > MAIN * P):
                def load_whole(e):
                    for p in range(2):
                        sp.dma_start(raw[p][:], expert_piece(e, p).rearrange("(c p) f -> p c f", p=P)
                                     ).then_inc(o_w_in, 16)
                    src = expert_piece(e, DOWN)
                    sp.dma_start(raw[DOWN][:, 0:KF - 1, :],
                                 src[0:(KF - 1) * P, :].rearrange("(c p) d -> p c d", p=P)).then_inc(o_w_in, 16)
                    sp.dma_start(raw[DOWN][0:FR, KF - 1, :], src[(KF - 1) * P:F, :]).then_inc(o_w_in, 16)

                load_whole(0)
                with sp.Fori(1, E) as e:
                    sp.wait_ge(o_down, REST * e)
                    load_whole(e)
                sp.wait_ge(o_added, 16 * REST * E)
            sp.dma_start(out_rows, acc_dram[0:T, :]).then_inc(out_done, 16)
            sp.wait_ge(out_done, 16)

        @block.gpsimd
        def _(pool):
            for q in range(2):
                pool.memset(A["xn"][q][:], 0.0).then_inc(consts_done, 1)
            pool.memset(ident[:], 0.0).then_inc(consts_done, 1)
            pool.memset(ones_bf[:], 1.0).then_inc(consts_done, 1)
            pool.memset(A["minus_half"][:], -0.5).then_inc(consts_done, 1)
            pool.wait_ge(consts_done, 5)
            pool.affine_select(out=ident[:], in_=ident[:], compare_op=ALU.not_equal, fill=1.0, base=0,
                               pattern=[[-1, P]], channel_multiplier=1).then_inc(consts_done, 1)
            pool.affine_select(out=before[:], in_=ones_bf[:], compare_op=ALU.is_gt, fill=0.0, base=0,
                               pattern=[[1, P]], channel_multiplier=-1).then_inc(iota_done, 1)
            pool.iota(iota_e[:], [[1, E]], base=0, channel_multiplier=0,
                      allow_small_or_imprecise_dtypes=True).then_inc(iota_done, 1)
            pool.iota(iota_a[:], [[1, NBLK]], base=0, channel_multiplier=0,
                      allow_small_or_imprecise_dtypes=True).then_inc(iota_done, 1)
            pool.iota(iota_s[:], [[1, P]], base=0, channel_multiplier=0,
                      allow_small_or_imprecise_dtypes=True).then_inc(iota_done, 1)
            pool.iota(fixed3[:, :, 1], [[1, NT]], base=0, channel_multiplier=0,
                      allow_small_or_imprecise_dtypes=True).then_inc(iota_done, 1)
            pool.iota(fixed3[:, :, 2], [[0, NT]], base=0, channel_multiplier=1,
                      allow_small_or_imprecise_dtypes=True).then_inc(iota_done, 1)
            pool.memset(fixed3[:, :, 0], 1.0).then_inc(iota_done, 1)
            pool.iota(trash_row[:], [[0, 1]], base=TRASH, channel_multiplier=1,
                      allow_small_or_imprecise_dtypes=True).then_inc(iota_done, 1)
            pool.iota(neg_trash_row[:], [[0, 1]], base=-TRASH, channel_multiplier=-1,
                      allow_small_or_imprecise_dtypes=True).then_inc(iota_done, 1)

            def inv_std(k, lo, n):
                pool.wait_ge(stats_done, k + 1)
                pool.nop(nofuse=True)
                pool.tensor_scalar(A["ve"][:, lo:lo + n], A["mv"][:, lo:lo + n, 1], EPS, None, ALU.add
                                   ).then_inc(rstd_link, 1)
                pool.tensor_scalar(A["neg_mean"][:, lo:lo + n], A["mv"][:, lo:lo + n, 0], -1.0, None, ALU.mult
                                   ).then_inc(rstd_link, 1)
                pool.wait_ge(rstd_link, 3 * k + 2)
                pool.tensor_tensor(A["rstd"][:, lo:lo + n], A["ve"][:, lo:lo + n], A["minus_half"][:, 0:n],
                                   ALU.pow).then_inc(rstd_link, 1)
                pool.wait_ge(rstd_link, 3 * k + 3)
                pool.tensor_tensor(A["shift"][:, lo:lo + n], A["neg_mean"][:, lo:lo + n], A["rstd"][:, lo:lo + n],
                                   ALU.mult).then_inc(rstd_done, 1)

            inv_std(0, 0, LT)
            with pool.Fori(0, B - 1) as b:
                inv_std(b * (1 + LT) + 1, 0, LT)
                for lt in range(LT):
                    inv_std(b * (1 + LT) + 2 + lt, LT + lt, 1)
            for lt in range(LT):
                inv_std((B - 1) * (1 + LT) + 1 + lt, LT + lt, 1)

            def free_xg(X):
                pool.wait_ge(xT_psum, X - 1)

            def load_xg(X, par):
                pool.dma_start(S["xg"][par][:], xn_dram[bass.ds(X * P, P), :]).then_inc(xg_in[par], 16)

            pool.wait_ge(tp_lo, UNITS)
            for q in range(2):
                pool.wait_ge(xn_stored[q], 16 * (1 + NT // 2))
            pool.wait_ge(logit_psum, NT)
            load_xg(0, 0)
            load_xg(1, 1)
            with pool.Fori(1, NT // 2) as i:
                for par in range(2):
                    free_xg(2 * i + par)
                    load_xg(2 * i + par, par)

            def index(r, k, e, j):
                pool.tensor_copy(S["idx"][k][:], S["row_tab"][:, bass.ds(e * NBLK + j, 1)]).then_inc(idx_done, 1)

            def gather(r, k):
                pool.wait_ge(idx_done, r + 1)
                free_xg(NT + r)
                pool.nop(nofuse=True)
                pool.indirect_dma_start(out=S["xg"][k % 2][:], out_offset=None, in_=xn_dram,
                                        in_offset=bass.IndirectOffsetOnAxis(ap=S["idx"][k][:], axis=0)
                                        ).then_inc(xg_in[k % 2], 16)

            pool.wait_ge(tab_done, 1)
            for k in range(2):
                index(k, k, 0, k)
                gather(k, k)
            pool.wait_ge(tab_done, E // 4)

            def pool_pair(i, first, last):
                r0 = 2 * MAIN * i
                for k in range(2 * MAIN):
                    r = r0 + k
                    if not (last and k >= 2 * MAIN - 2):
                        kk = (k + 2) % (2 * MAIN)
                        e2 = 2 * i + (k + 2) // MAIN
                        index(r + 2, kk, e2, (k + 2) % MAIN)
                        gather(r + 2, kk)
                    if not (first and k == 0):
                        scatter_at(i, k - 1, first)
                if last:
                    scatter_at(i, 2 * MAIN - 1, first)

            def scatter_at(i, k, first):
                if k < 0:
                    i, k = i - 1, 2 * MAIN - 1
                r0 = 2 * MAIN * i
                pool.wait_ge(y_scaled, r0 + k + 1)
                if first and k == 0:
                    pool.wait_ge(acc_written, 16 * NT)
                else:
                    pool.wait_ge(added[(k + 1) % 2], 16 * (MAIN * i) + 16 * ((k + 1) // 2))
                pool.nop(nofuse=True)
                pool.indirect_dma_start(out=acc_dram, in_=S["ys"][k % 2][:], in_offset=None,
                                        out_offset=bass.IndirectOffsetOnAxis(ap=S["idx"][k][:], axis=0),
                                        compute_op=ALU.add).then_inc(added[k % 2], 16)

            pool_pair(0, True, False)
            with pool.Fori(1, E // 2 - 1) as i:
                pool_pair(i, False, False)
            pool_pair(E // 2 - 1, False, True)

            main_added(pool)
            with pool.If(most_rows(pool) > MAIN * P):
                with pool.Fori(0, E) as e:
                    for j in range(REST):
                        q = REST * e + j
                        pool.tensor_copy(S["idx"][0][:], S["row_tab"][:, bass.ds(e * NBLK + MAIN + j, 1)]
                                         ).then_inc(o_idx, 1)
                        pool.wait_ge(o_idx, q + 1)
                        pool.nop(nofuse=True)
                        pool.indirect_dma_start(out=o_x[:], out_offset=None, in_=xn_dram,
                                                in_offset=bass.IndirectOffsetOnAxis(ap=S["idx"][0][:], axis=0)
                                                ).then_inc(o_x_in, 16)
                        pool.wait_ge(o_scaled, q + 1)
                        pool.nop(nofuse=True)
                        pool.indirect_dma_start(out=acc_dram, in_=o_y[:], in_offset=None,
                                                out_offset=bass.IndirectOffsetOnAxis(ap=S["idx"][0][:], axis=0),
                                                compute_op=ALU.add).then_inc(o_added, 16)
                        pool.wait_ge(o_added, 16 * (q + 1))

        @block.scalar
        def _(act):
            act.wait_ge(small_loaded, 16 * 7)
            act.activation(tanh_g[:], g_raw[:], ACT.Tanh).then_inc(tanh_done, 1)

            def round_unit(u, par, dst, cols=512, shape=None):
                act.wait_ge(tp_psum, u + 1)
                src = bank[par][:, 0:cols]
                act.activation(dst, src if shape is None else shape(src), ACT.Copy).then_inc(tp_hi, 1)

            chunks = lambda v: v.rearrange("p (c t) -> p c t", t=P)
            round_unit(0, 0, A["wqkT"][0][:].rearrange("p a c d -> p (a c) d"), shape=chunks)
            round_unit(1, 1, A["routT"][0][:], KD * E, lambda v: v.rearrange("p (c e) -> p c e", e=E))

            def weight_hi(n, slot, p, after_gu=None, after_down=None):
                act.wait_ge(raw_in[p], 16 * (n + 1) if p < DOWN else 32 * (n + 1))
                if p < DOWN and after_gu is not None:
                    act.wait_ge(gu_done, after_gu)
                if p == DOWN and after_down is not None:
                    act.wait_ge(down_done, after_down)
                if p < DOWN:
                    act.activation(w_hi[slot][p][:], raw[p][:], ACT.Copy).then_inc(w_hi_done, 1)
                else:
                    act.activation(w_hi[slot][p][:, 0:KF - 1, :], raw[p][:, 0:KF - 1, :], ACT.Copy
                                   ).then_inc(w_hi_done, 1)
                    act.activation(w_hi[slot][p][0:FR, KF - 1, :], raw[p][0:FR, KF - 1, :], ACT.Copy
                                   ).then_inc(w_hi_done, 1)

            def act_round(f, b, n):
                R = Round(f, b)

                def turned(name, dst, shape=chunks):
                    if name in R.turns:
                        round_unit(*R.unit(name), dst, shape=shape)

                def ctx_hi(c):
                    turned(f"ctx{c}", A["ctxT"][0][:, c, :], None)

                def qk_hi_part(j):
                    if f is None:
                        return
                    act.wait_ge(qk_psum, 2 * f + j + 1)
                    act.activation(A["qkT"][0][:, j, :], bank[2 + j][:], ACT.Identity, bias=A["b_qk"][:, j:j + 1]
                                   ).then_inc(qk_hi, 1)

                def norm_x(lt):
                    if f is None:
                        return
                    act.wait_ge(rstd_done, (1 + LT) * f - (LT if not isinstance(f, int) or f else 0) + 1)
                    act.activation(A["xl"][:, lt, :], x_sb[:, bass.ds(f * LT + lt, 1), :].rearrange("p a d -> p (a d)"),
                                   ACT.Identity, bias=A["shift"][:, lt:lt + 1], scale=A["rstd"][:, lt:lt + 1]
                                   ).then_inc(xl_done, 1)

                def soft(mt):
                    if f is None:
                        return
                    act.wait_ge(max_done, f * LT + mt + 1)
                    if mt >= 2:
                        act.wait_ge(tp_psum, R.unit(f"att{mt - 2}")[0] + 1)
                    act.activation(A["prob"][mt % 2][:], bank[4 + mt % 2][:], ACT.Exp,
                                   bias=A["neg_max"][:, mt:mt + 1], accum_out=A["psum_row"][:, mt:mt + 1]
                                   ).then_inc(exp_done, 1)

                def norm_prob(mt):
                    if f is None:
                        return
                    act.wait_ge(recip_done, f * LT + mt + 1)
                    act.activation(A["prob"][mt % 2][:], A["prob"][mt % 2][:], ACT.Copy,
                                   scale=A["r_row"][:, mt:mt + 1]).then_inc(prob_done, 1)

                def norm_x2(lt):
                    if b is None:
                        return
                    act.wait_ge(rstd_done, b * (1 + LT) + 3 + lt - (1 if f is None else 0))
                    act.wait_ge(xn_stored[lt % 2], 16 * (1 + (LT // 2) * b + lt // 2))
                    act.activation(A["xn"][lt % 2][:], x_sb[:, bass.ds(b * LT + lt, 1), :].rearrange("p a d -> p (a d)"),
                                   ACT.Identity, bias=A["shift"][:, LT + lt:LT + lt + 1],
                                   scale=A["rstd"][:, LT + lt:LT + lt + 1]).then_inc(xn_done, 1)

                def keep_logit(lt):
                    if b is None:
                        return
                    act.wait_ge(logit_psum, b * LT + lt + 1)
                    act.activation(A["logit"][:, lt, :], bank[2 + lt % 2][:, 0:E], ACT.Copy).then_inc(logit_done, 1)

                def route_exp(lt):
                    if b is None:
                        return
                    tile = b * LT + lt
                    act.wait_ge(top_done, tile + 1)
                    act.activation(expd[:, bass.ds(tile, 1), :].rearrange("p a e -> p (a e)"), A["logit"][:, lt, :],
                                   ACT.Exp, bias=A["neg_top"][:, lt:lt + 1], accum_out=denom[:, bass.ds(tile, 1)]
                                   ).then_inc(rexp_done, 1)

                def xn_hi(lt):
                    turned(f"xn{lt}", A["xnT"][0][lt % 2][:])

                def x_hi(lt):
                    turned(f"x{lt}", A["xlT"][0][:, lt, :, :])

                def att_hi(mt):
                    turned(f"att{mt}", A["attT"][0][:, :, mt * P:(mt + 1) * P])

                def weights(p):
                    if n is not None:
                        weight_hi(n, n, p)

                ctx_hi(0)
                ctx_hi(1)
                norm_x(0)
                norm_x(1)
                qk_hi_part(0)
                qk_hi_part(1)
                norm_x2(0)
                soft(0)
                xn_hi(0)
                soft(1)
                x_hi(0)
                norm_prob(0)
                norm_prob(1)
                norm_x2(1)
                keep_logit(0)
                weights(0)
                x_hi(1)
                norm_x(2)
                norm_x(3)
                att_hi(0)
                soft(2)
                norm_x2(2)
                xn_hi(1)
                att_hi(1)
                soft(3)
                x_hi(2)
                keep_logit(1)
                norm_prob(2)
                norm_x2(3)
                weights(1)
                xn_hi(2)
                norm_prob(3)
                x_hi(3)
                keep_logit(2)
                att_hi(2)
                xn_hi(3)
                keep_logit(3)
                weights(2)
                for lt in range(LT):
                    route_exp(lt)
                att_hi(3)

            act_round(0, None, 0)
            with act.Fori(0, B - 1) as b:
                act_round(b + 1, b, None)
            act_round(None, B - 1, 1)

            def do_silu(g):
                act.wait_ge(gu_done, g + 1)
                if not (isinstance(g, int) and g == 0):
                    act.wait_ge(h_done, g)
                act.activation(S["silu"][:], bank[1][:, 0:F], ACT.Silu).then_inc(silu_done, 1)

            def xT_hi_part(X, par):
                act.wait_ge(xT_psum, X + 1)
                act.activation(S["xT"][0][par][:], chunks(bank[0][:]), ACT.Copy).then_inc(xT_hi, 1)

            def hT_hi_part(g):
                act.wait_ge(hT_psum, g + 1)
                src = chunks(bank[3][:, 0:KF * P])
                act.activation(S["hT"][0][:, 0:KF - 1, :], src[:, 0:KF - 1, :], ACT.Copy).then_inc(hT_hi, 1)
                act.activation(S["hT"][0][0:FR, KF - 1, :], src[0:FR, KF - 1, :], ACT.Copy).then_inc(hT_hi, 1)

            def scale_y(i, k):
                if k < 0:
                    i, k = i - 1, 2 * MAIN - 1
                r = 2 * MAIN * i + k
                act.wait_ge(down_done, SH + r + 1)
                if not (isinstance(i, int) and i == 0 and k < 2):
                    act.wait_ge(added[k % 2], 16 * MAIN * i + 16 * (k // 2))
                act.activation(S["ys"][k % 2][:], bank[4][:], ACT.Copy,
                               scale=S["w_tab"][:, bass.ds((2 * i + k // MAIN) * NBLK + k % MAIN, 1)]
                               ).then_inc(y_scaled, 1)

            act.wait_ge(tp_lo, UNITS)
            act.wait_ge(logit_psum, NT)
            for X in range(1):
                xT_hi_part(0, 0)

            def act_shared(i, last):
                for j in range(4):
                    g = 4 * i + j
                    do_silu(g)
                    if j % 2 == 1:
                        xT_hi_part(2 * i + j // 2 + 1, (j // 2 + 1) % 2)
                    if last and j == 3:
                        for p in range(2):
                            weight_hi(2, 0, p, after_gu=SH - 1)
                    hT_hi_part(g)
                    if last and j == 3:
                        weight_hi(2, 0, DOWN, after_down=SH - 1)

            act_shared(0, False)
            with act.Fori(1, SH // 4 - 1) as i:
                act_shared(i, False)
            act_shared(SH // 4 - 1, True)

            act.wait_ge(tab_done, E // 4)

            def act_pair(i, first, last):
                for k in range(2 * MAIN):
                    r = 2 * MAIN * i + k
                    do_silu(SH + r)
                    if not (last and k == 2 * MAIN - 1):
                        xT_hi_part(NT + r + 1, (k + 1) % 2)
                    if not (first and k == 0):
                        scale_y(i, k - 1)
                    hT_hi_part(SH + r)
                    j = k % MAIN
                    e = 2 * i + k // MAIN
                    if j >= 1 and not (last and k >= MAIN):
                        weight_hi(e + 3, (k // MAIN + 1) % 2, j - 1, after_gu=SH + MAIN * e, after_down=SH + MAIN * e)
                if last:
                    scale_y(i, 2 * MAIN - 1)

            act_pair(0, True, False)
            with act.Fori(1, E // 2 - 1) as i:
                act_pair(i, False, False)
            act_pair(E // 2 - 1, False, True)

            main_added(act)
            with act.If(most_rows(act) > MAIN * P):
                with act.Fori(0, E) as e:
                    for j in range(REST):
                        q = REST * e + j
                        act.wait_ge(o_x_psum, q + 1)
                        act.activation(o_xT_sb, chunks(bank[0][:]), ACT.Copy).then_inc(o_xT, 1)
                        act.wait_ge(o_gu, q + 1)
                        act.activation(S["silu"][:], bank[1][:, 0:F], ACT.Silu).then_inc(o_silu, 1)
                        act.wait_ge(o_h_psum, q + 1)
                        src = chunks(bank[3][:, 0:KF * P])
                        act.activation(o_hT_sb[:, 0:KF - 1, :], src[:, 0:KF - 1, :], ACT.Copy).then_inc(o_hT, 1)
                        act.activation(o_hT_sb[0:FR, KF - 1, :], src[0:FR, KF - 1, :], ACT.Copy).then_inc(o_hT, 1)
                        act.wait_ge(o_down, q + 1)
                        act.activation(o_y[:], bank[4][:], ACT.Copy,
                                       scale=S["w_tab"][:, bass.ds(e * NBLK + MAIN + j, 1)]).then_inc(o_scaled, 1)
                act.wait_ge(o_scaled, REST * E)

        @block.vector
        def _(dve):
            chunks = lambda v: v.rearrange("p (c t) -> p c t", t=P)

            def rest_unit(u, par, hi, lo, cols=512, shape=None):
                dve.wait_ge(tp_hi, u + 1)
                src = bank[par][:, 0:cols]
                dve.tensor_tensor(lo, src if shape is None else shape(src), hi, ALU.subtract).then_inc(tp_lo, 1)

            rest_unit(0, 0, A["wqkT"][0][:].rearrange("p a c d -> p (a c) d"),
                      A["wqkT"][1][:].rearrange("p a c d -> p (a c) d"), shape=chunks)
            rest_unit(1, 1, A["routT"][0][:], A["routT"][1][:], KD * E, lambda v: v.rearrange("p (c e) -> p c e", e=E))

            def weight_lo(n, slot, p):
                if p < DOWN:
                    dve.wait_ge(w_hi_done, 4 * n + p + 1)
                    dve.tensor_tensor(w_lo[slot][p][:], raw[p][:], w_hi[slot][p][:], ALU.subtract
                                      ).then_inc(w_ready, 1)
                else:
                    dve.wait_ge(w_hi_done, 4 * n + 4)
                    dve.tensor_tensor(w_lo[slot][p][:, 0:KF - 1, :], raw[p][:, 0:KF - 1, :],
                                      w_hi[slot][p][:, 0:KF - 1, :], ALU.subtract)
                    dve.tensor_tensor(w_lo[slot][p][0:FR, KF - 1, :], raw[p][0:FR, KF - 1, :],
                                      w_hi[slot][p][0:FR, KF - 1, :], ALU.subtract).then_inc(w_ready, 1)

            def dve_round(f, b, n):
                R = Round(f, b)

                def turned(name, hi, lo, shape=chunks):
                    if name in R.turns:
                        rest_unit(*R.unit(name), hi, lo, shape=shape)

                def ctx_lo(c):
                    turned(f"ctx{c}", A["ctxT"][0][:, c, :], A["ctxT"][1][:, c, :], None)

                def xn_lo(lt):
                    turned(f"xn{lt}", A["xnT"][0][lt % 2][:], A["xnT"][1][lt % 2][:])

                def x_lo(lt):
                    turned(f"x{lt}", A["xlT"][0][:, lt, :, :], A["xlT"][1][:, lt, :, :])

                def att_lo(mt):
                    turned(f"att{mt}", A["attT"][0][:, :, mt * P:(mt + 1) * P], A["attT"][1][:, :, mt * P:(mt + 1) * P])

                stats_before = (LT * f + LT * f - LT if not isinstance(f, int) or f else 0) if f is not None else None

                def stats_x():
                    if f is None:
                        return
                    for lt in range(LT):
                        dve.bn_stats(A["stats"][:, lt, :],
                                     x_sb[:, bass.ds(f * LT + lt, 1), :].rearrange("p a d -> p (a d)")
                                     ).then_inc(stat_link, 1)
                    dve.wait_ge(stat_link, stats_before + LT)
                    dve.nop(nofuse=True)
                    for lt in range(LT):
                        ins = dve.bn_aggr(A["mv"][:, lt, :], A["stats"][:, lt, :])
                    ins.then_inc(stats_done, 1)

                def qk_lo_part(j):
                    if f is None:
                        return
                    dve.wait_ge(qk_hi, 2 * f + j + 1)
                    dve.scalar_tensor_tensor(A["qkT"][1][:, j, :], bank[2 + j][:], A["b_qk"][:, j:j + 1],
                                             A["qkT"][0][:, j, :].bitcast(F32), ALU.add, ALU.subtract).then_inc(qk_lo, 1)

                def row_max(mt):
                    if f is None:
                        return
                    dve.wait_ge(energy_done, f * LT + mt + 1)
                    dve.tensor_reduce(A["neg_max"][:, mt:mt + 1], bank[4 + mt % 2][:], AX, ALU.max, negate=True
                                      ).then_inc(max_done, 1)

                def recip(mt):
                    if f is None:
                        return
                    dve.wait_ge(exp_done, f * LT + mt + 1)
                    dve.reciprocal(A["r_row"][:, mt:mt + 1], A["psum_row"][:, mt:mt + 1]).then_inc(recip_done, 1)

                def add_attended(lt):
                    if b is None:
                        return
                    tile = b * LT + lt
                    row = x_sb[:, bass.ds(tile, 1), :].rearrange("p a d -> p (a d)")
                    dve.wait_ge(attend_done, tile + 1)
                    dve.scalar_tensor_tensor(row, bank[6 + lt % 2][:], tanh_g[:, 0:1], row, ALU.mult, ALU.add
                                             ).then_inc(x2_done, 1)
                    dve.wait_ge(x2_done, tile + 1)
                    dve.nop(nofuse=True)
                    dve.bn_stats(A["stats"][:, LT + lt, :], row).then_inc(stat_link, 1)
                    dve.wait_ge(stat_link, LT * (b + 2) + LT * b + lt + 1 if f is not None else LT * B + LT * b + lt + 1)
                    dve.nop(nofuse=True)
                    dve.bn_aggr(A["mv"][:, LT + lt, :], A["stats"][:, LT + lt, :]).then_inc(stats_done, 1)

                def best(lt):
                    if b is None:
                        return
                    dve.wait_ge(logit_done, b * LT + lt + 1)
                    dve.nop(nofuse=True)
                    dve.max(A["top8"][:, lt, :], A["logit"][:, lt, :]).then_inc(top_link, 1)
                    dve.wait_ge(top_link, b * LT + lt + 1)
                    dve.nop(nofuse=True)
                    dve.max_index(A["top_at"][:, lt, :], A["top8"][:, lt, :], A["logit"][:, lt, :]
                                  ).then_inc(index_done, 1)
                    dve.tensor_scalar(A["neg_top"][:, lt:lt + 1], A["top8"][:, lt, 0:1], -1.0, None, ALU.mult
                                      ).then_inc(top_done, 1)

                def keep_top():
                    if b is None:
                        return
                    dve.wait_ge(index_done, (b + 1) * LT)
                    dve.tensor_copy(top_f[:, bass.ds(b * LT, LT), :], A["top_at"][:]).then_inc(top_kept, 1)

                def weights(p):
                    if n is not None:
                        weight_lo(n, n, p)

                if b is None:
                    stats_x()
                ctx_lo(0)
                ctx_lo(1)
                if b is not None:
                    stats_x()
                add_attended(0)
                qk_lo_part(0)
                qk_lo_part(1)
                add_attended(1)
                row_max(0)
                row_max(1)
                xn_lo(0)
                recip(0)
                recip(1)
                x_lo(0)
                add_attended(2)
                best(0)
                weights(0)
                x_lo(1)
                row_max(2)
                add_attended(3)
                att_lo(0)
                recip(2)
                xn_lo(1)
                att_lo(1)
                row_max(3)
                x_lo(2)
                recip(3)
                best(1)
                weights(1)
                xn_lo(2)
                x_lo(3)
                best(2)
                att_lo(2)
                xn_lo(3)
                best(3)
                weights(2)
                keep_top()
                att_lo(3)

            dve.wait_ge(x_in[0], 16)
            dve_round(0, None, 0)
            for q in range(1, B):
                dve.wait_ge(x_in[q], 16)
            with dve.Fori(0, B - 1) as b:
                dve_round(b + 1, b, None)
            dve_round(None, B - 1, 1)

            step = [0]

            def link(ins):
                step[0] += 1
                ins.then_inc(route, 1)
                dve.wait_ge(route, step[0])

            dve.wait_ge(rexp_done, NT)
            dve.wait_ge(logit_psum, NT)
            for q in range(2):
                dve.wait_ge(xn_stored[q], 16 * (1 + NT // 2))
            dve.wait_ge(iota_done, 9)
            over_e = lambda v: v[:].rearrange("p (t a) -> p t a", a=1).to_broadcast([P, NT, E])
            dve.wait_ge(top_kept, B)
            iota_all = iota_e[:].rearrange("p (a e) -> p a e", a=1).to_broadcast([P, NT, E])
            for k in range(TOPK):
                at_k = top_f[:, :, k:k + 1].to_broadcast([P, NT, E])
                link(dve.tensor_tensor(S["mask" if k == 0 else "hit"][:], iota_all, at_k, ALU.is_equal))
                if k:
                    link(dve.tensor_tensor(S["mask"][:], S["mask"][:], S["hit"][:], ALU.add))
            dve.tensor_copy(S["mask_bf"][:], S["mask"][:]).then_inc(mask_ready, 1)
            link(dve.reciprocal(S["rz"][:], denom[:]))
            link(dve.tensor_tensor(S["score"][:], expd[:], over_e(S["rz"]), ALU.mult))
            link(dve.tensor_tensor(S["score"][:], S["score"][:], S["mask"][:], ALU.mult))
            link(dve.tensor_reduce(S["tsum"][:], S["score"][:], AX, ALU.add))
            link(dve.tensor_scalar(S["tsum"][:], S["tsum"][:], 1e-20, None, ALU.add))
            link(dve.reciprocal(S["trec"][:], S["tsum"][:]))
            link(dve.tensor_tensor(S["score"][:], S["score"][:], over_e(S["trec"]), ALU.mult))
            for part in range(3):
                link(dve.tensor_copy(S["w3"][:, :, :, part], S["score"][:]))
                if part < 2:
                    link(dve.tensor_tensor(S["score"][:], S["score"][:], S["w3"][:, :, :, part], ALU.subtract))
            dve.wait_ge(ranked, 1)
            ranks = bank[6][:].rearrange("p (t e) -> p t e", e=E)
            link(dve.scalar_tensor_tensor(S["rank"][:], S["mask"][:], float(-4 * T), ranks, ALU.mult, ALU.add))
            link(dve.tensor_scalar(S["rank_i"][:], S["rank"][:], float(4 * T), None, ALU.add))
            link(dve.tensor_scalar(S["blk_i"][:], S["rank_i"][:], 7, None, ALU.arith_shift_right))
            link(dve.tensor_scalar(S["rank_i"][:], S["rank_i"][:], P - 1, None, ALU.bitwise_and))
            link(dve.tensor_copy(S["blk"][:], S["blk_i"][:]))
            link(dve.tensor_copy(S["pos"][:], S["rank_i"][:]))
            link(dve.tensor_reduce(S["most"][:], bank[7][:, 0:E], AX, ALU.max))
            dve.tensor_copy(S["most_i"][:], S["most"][:]).then_inc(most_ready, 1)

            def make_h(g):
                dve.wait_ge(silu_done, g + 1)
                if not (isinstance(g, int) and g == 0):
                    dve.wait_ge(hT_psum, g)
                dve.tensor_tensor(S["h"][:], bank[2][:, 0:F], S["silu"][:], ALU.mult).then_inc(h_done, 1)

            def xT_lo_part(X, par):
                dve.wait_ge(xT_hi, X + 1)
                dve.tensor_tensor(S["xT"][1][par][:], chunks(bank[0][:]), S["xT"][0][par][:], ALU.subtract
                                  ).then_inc(xT_lo, 1)

            def hT_lo_part(g):
                dve.wait_ge(hT_hi, 2 * g + 2)
                src = chunks(bank[3][:, 0:KF * P])
                dve.tensor_tensor(S["hT"][1][:, 0:KF - 1, :], src[:, 0:KF - 1, :], S["hT"][0][:, 0:KF - 1, :],
                                  ALU.subtract)
                dve.tensor_tensor(S["hT"][1][0:FR, KF - 1, :], src[0:FR, KF - 1, :], S["hT"][0][0:FR, KF - 1, :],
                                  ALU.subtract).then_inc(hT_lo, 1)

            def add_shared(t):
                dve.wait_ge(down_done, 2 * t + 2)
                row = x_sb[:, bass.ds(t, 1), :].rearrange("p a d -> p (a d)")
                dve.scalar_tensor_tensor(row, bank[4][:], tanh_g[:, 1:2], row, ALU.mult, ALU.add
                                         ).then_inc(shared_added, 1)

            def table_values(e, par, first):
                if not first:
                    dve.wait_ge(tab_psum, e - 1)
                blk_e = S["blk"][:, :, bass.ds(e, 1)].to_broadcast([P, NT, NBLK])
                a_all = iota_a[:].rearrange("p (o a) -> p o a", o=1).to_broadcast([P, NT, NBLK])
                dve.tensor_tensor(S["in_blk"][:], a_all, blk_e, ALU.is_equal).then_inc(in_blk_done, 1)
                pos_e = S["pos"][:, :, bass.ds(e, 1)].to_broadcast([P, NT, P])
                s_all = iota_s[:].rearrange("p (a s) -> p a s", a=1).to_broadcast([P, NT, P])
                dve.tensor_tensor(S["onehot"][par][:], s_all, pos_e, ALU.is_equal)
                dve.wait_ge(in_blk_done, e + 1)
                in4 = S["in_blk"][:].rearrange("p t (o a) -> p t o a", o=1).to_broadcast([P, NT, 3, NBLK])
                f4 = fixed3[:].rearrange("p t (v o) -> p t v o", o=1).to_broadcast([P, NT, 3, NBLK])
                w4 = S["w3"][:, :, bass.ds(e, 1), :].rearrange("p t o v -> p t v o").to_broadcast([P, NT, 3, NBLK])
                dve.tensor_tensor(S["vals"][par][:, :, 0:3, :], in4, f4, ALU.mult)
                dve.tensor_tensor(S["vals"][par][:, :, 3:6, :], in4, w4, ALU.mult).then_inc(vals_done, 1)

            def finish_tables(i):
                dve.wait_ge(tab_psum, 4 * i + 4)
                tab = S["tab"]
                dve.tensor_copy(tab[:].rearrange("p e v a -> p (e v a)"), bank[5][:, 0:4 * NV * NBLK]
                                ).then_inc(tab_copied, 1)
                dve.wait_ge(tab_copied, i + 1)
                dve.scalar_tensor_tensor(S["t1"][:], tab[:, :, 1, :], float(P), tab[:, :, 2, :], ALU.mult, ALU.add
                                         ).then_inc(tab_link, 1)
                dve.tensor_tensor(S["u1"][:], tab[:, :, 3, :], tab[:, :, 4, :], ALU.add).then_inc(tab_link, 1)
                dve.wait_ge(tab_link, 4 * i + 1)
                dve.scalar_tensor_tensor(S["t2"][:], tab[:, :, 0, :], neg_trash_row[:, 0:1], S["t1"][:], ALU.mult,
                                         ALU.add).then_inc(tab_link, 1)
                dve.wait_ge(tab_link, 4 * i + 2)
                dve.tensor_tensor(S["u2"][:], S["u1"][:], tab[:, :, 5, :], ALU.add).then_inc(tab_link, 1)
                dve.wait_ge(tab_link, 4 * i + 3)
                flat = lambda v: v[:].rearrange("p e a -> p (e a)")
                dve.tensor_scalar(S["row_tab"][:, bass.ds(4 * NBLK * i, 4 * NBLK)], flat(S["t2"]), trash_row[:, 0:1],
                                  None, ALU.add)
                dve.wait_ge(tab_link, 4 * i + 4)
                dve.tensor_scalar(S["w_tab"][:, bass.ds(4 * NBLK * i, 4 * NBLK)], flat(S["u2"]), tanh_g[:, 1:2],
                                  None, ALU.mult).then_inc(tab_done, 1)

            xT_lo_part(0, 0)

            def dve_shared(i, first, last):
                for j in range(4):
                    g = 4 * i + j
                    make_h(g)
                    if j % 2 == 1:
                        xT_lo_part(2 * i + j // 2 + 1, (j // 2 + 1) % 2)
                    elif not (first and j == 0):
                        add_shared(2 * i + j // 2 - 1)
                    if last and j == 3:
                        for p in range(2):
                            weight_lo(2, 0, p)
                    hT_lo_part(g)
                    if last and j == 3:
                        weight_lo(2, 0, DOWN)
                    if j == 0 and not first:
                        finish_tables(i - 1)
                    table_values(g, j % 2, first and j < 2)

            dve_shared(0, True, False)
            with dve.Fori(1, SH // 4 - 1) as i:
                dve_shared(i, False, False)
            dve_shared(SH // 4 - 1, False, True)
            finish_tables(SH // 4 - 1)

            def dve_pair(i, first, last):
                for k in range(2 * MAIN):
                    r = 2 * MAIN * i + k
                    make_h(SH + r)
                    if first and k == 0:
                        add_shared(NT - 1)
                    if not (last and k == 2 * MAIN - 1):
                        xT_lo_part(NT + r + 1, (k + 1) % 2)
                    hT_lo_part(SH + r)
                    j = k % MAIN
                    e = 2 * i + k // MAIN
                    if j >= 1 and not (last and k >= MAIN):
                        weight_lo(e + 3, (k // MAIN + 1) % 2, j - 1)

            dve_pair(0, True, False)
            with dve.Fori(1, E // 2 - 1) as i:
                dve_pair(i, False, False)
            dve_pair(E // 2 - 1, False, True)

            main_added(dve)
            with dve.If(most_rows(dve) > MAIN * P):
                with dve.Fori(0, REST * E) as q:
                    dve.wait_ge(o_silu, q + 1)
                    dve.tensor_tensor(S["h"][:], bank[2][:, 0:F], S["silu"][:], ALU.mult).then_inc(o_h, 1)
                dve.wait_ge(o_h, REST * E)

        @block.tensor
        def _(pe):
            def product(ps, lhs, rhs, start, stop):
                pe.matmul(ps, lhs[0], rhs[0], start=start, stop=False)
                pe.matmul(ps, lhs[0], rhs[1], start=False, stop=False)
                return pe.matmul(ps, lhs[1], rhs[0], start=False, stop=stop)

            def unit_free(u):
                pe.wait_ge(tp_lo, u - 1)

            pe.wait_ge(consts_done, 6)
            pe.wait_ge(small_loaded, 16 * 7)
            for a in range(2):
                for c in range(KC):
                    ins = pe.transpose(bank[0][:, (a * KC + c) * P:(a * KC + c + 1) * P],
                                       A["wqk"][:, a, c * P:(c + 1) * P], ident[:])
            ins.then_inc(tp_psum, 1)
            for c in range(KD):
                ins = pe.transpose(bank[1][:, c * E:(c + 1) * E], A["rout"][:, c * P:(c + 1) * P], ident[0:E, 0:E])
            ins.then_inc(tp_psum, 1)

            def pe_round(f, b):
                R = Round(f, b)

                def turn(name, parts):
                    u, par = R.unit(name)
                    unit_free(u)
                    for k, part in enumerate(parts):
                        ins = pe.transpose(bank[par][:, k * P:(k + 1) * P], part, ident[:])
                    ins.then_inc(tp_psum, 1)

                def turn_ctx(c):
                    if f is None:
                        return
                    pe.wait_ge(ctx_loaded, 16 * (f + 1))
                    turn(f"ctx{c}", [A["ctx_sb"][:, t, c * P:(c + 1) * P] for t in range(LT)])

                def queries_keys():
                    if f is None:
                        return
                    pe.wait_ge(tp_lo, R.unit("ctx1")[0] + 1)
                    for a in range(2):
                        for c in range(KC):
                            ins = product(bank[2 + a][:], [A["wqkT"][s][:, a, c, :] for s in range(2)],
                                          [A["ctxT"][s][:, c, :] for s in range(2)], c == 0, c == KC - 1)
                        ins.then_inc(qk_psum, 1)

                def turn_x_rows(lt):
                    if f is None:
                        return
                    pe.wait_ge(xl_done, f * LT + lt + 1)
                    turn(f"x{lt}", [A["xl"][:, lt, c * P:(c + 1) * P] for c in range(KD)])

                def energy(mt):
                    if f is None:
                        return
                    if mt >= 2:
                        pe.wait_ge(exp_done, f * LT + mt - 1)
                    pe.wait_ge(qk_lo, 2 * f + 2)
                    product(bank[4 + mt % 2][:], [A["qkT"][s][:, 0, mt * P:(mt + 1) * P] for s in range(2)],
                            [A["qkT"][s][:, 1, :] for s in range(2)], True, True).then_inc(energy_done, 1)

                def turn_prob(mt):
                    if f is None:
                        return
                    pe.wait_ge(prob_done, f * LT + mt + 1)
                    turn(f"att{mt}", [A["prob"][mt % 2][:, c * P:(c + 1) * P] for c in range(KD)])

                def attend(lt):
                    if b is None:
                        return
                    if lt >= 2:
                        pe.wait_ge(x2_done, b * LT + lt - 1)
                    pe.wait_ge(tp_lo, R.base)
                    for c in range(KD):
                        ins = product(bank[6 + lt % 2][:], [A["xlT"][s][:, lt, c, :] for s in range(2)],
                                      [A["attT"][s][:, c, :] for s in range(2)], c == 0, c == KD - 1)
                    ins.then_inc(attend_done, 1)

                def turn_xn(lt):
                    if b is None:
                        return
                    pe.wait_ge(xn_done, b * LT + lt + 1)
                    turn(f"xn{lt}", [A["xn"][lt % 2][:, c * P:(c + 1) * P] for c in range(KD)])

                def logits(lt):
                    if b is None:
                        return
                    pe.wait_ge(tp_lo, R.unit(f"xn{lt}")[0] + 1)
                    if lt >= 2:
                        pe.wait_ge(logit_done, b * LT + lt - 1)
                    for c in range(KD):
                        ins = product(bank[2 + lt % 2][:, 0:E], [A["xnT"][s][lt % 2][:, c, :] for s in range(2)],
                                      [A["routT"][s][:, c, :] for s in range(2)], c == 0, c == KD - 1)
                    ins.then_inc(logit_psum, 1)

                turn_ctx(0)
                turn_ctx(1)
                attend(0)
                queries_keys()
                attend(1)
                energy(0)
                energy(1)
                turn_xn(0)
                turn_x_rows(0)
                attend(2)
                logits(0)
                turn_x_rows(1)
                energy(2)
                attend(3)
                turn_prob(0)
                turn_xn(1)
                energy(3)
                turn_prob(1)
                turn_x_rows(2)
                logits(1)
                turn_xn(2)
                turn_x_rows(3)
                logits(2)
                turn_prob(2)
                turn_xn(3)
                logits(3)
                turn_prob(3)

            pe_round(0, None)
            with pe.Fori(0, B - 1) as b:
                pe_round(b + 1, b)
            pe_round(None, B - 1)

            pe.wait_ge(mask_ready, 1)
            pe.wait_ge(x2_done, NT)
            flat = S["mask_bf"][:].rearrange("p t e -> p (t e)")
            pe.matmul(bank[6][:], before[:], flat, start=True, stop=True)
            for d in range(1, NT):
                pe.matmul(bank[6][:, d * E:], ones_bf[:], flat[:, 0:(NT - d) * E], start=False, stop=True,
                          skip_group_check=True)
            for t in range(NT):
                ins = pe.matmul(bank[7][:, 0:E], ones_bf[:], flat[:, t * E:(t + 1) * E], start=t == 0, stop=t == NT - 1)
            ins.then_inc(ranked, 1)

            def turn_x(X, par, count):
                pe.wait_ge(xg_in[par], 16 * count)
                if not (isinstance(X, int) and X == 0):
                    pe.wait_ge(xT_lo, X)
                for c in range(KD):
                    ins = pe.transpose(bank[0][:, c * P:(c + 1) * P], S["xg"][par][:, c * P:(c + 1) * P], ident[:])
                ins.then_inc(xT_psum, 1)

            def gate_up(n, slot, X, par):
                pe.wait_ge(xT_lo, X + 1)
                pe.wait_ge(w_ready, 3 * n + 2)
                for c in range(KD):
                    for s, parts in ((0, (w_hi, w_lo)), (1, (w_hi,))):
                        for w in parts:
                            for q in range(2):
                                first = c == 0 and s == 0 and w is w_hi
                                ins = pe.matmul(bank[1 + q][:, 0:F], S["xT"][s][par][:, c, :], w[slot][q][:, c, :],
                                                start=first, stop=c == KD - 1 and s == 1)
                ins.then_inc(gu_done, 1)

            def turn_h(g):
                pe.wait_ge(h_done, g + 1)
                if not (isinstance(g, int) and g == 0):
                    pe.wait_ge(hT_lo, g)
                for c in range(KF):
                    n = P if c < KF - 1 else FR
                    ins = pe.transpose(bank[3][0:n, c * P:(c + 1) * P], S["h"][:, c * P:c * P + n], ident[:])
                ins.then_inc(hT_psum, 1)

            def down(g, n, slot, start, stop):
                pe.wait_ge(hT_lo, g + 1)
                pe.wait_ge(w_ready, 3 * n + 3)
                for c in range(KF):
                    k = P if c < KF - 1 else FR
                    ins = product(bank[4][:], [S["hT"][s][0:k, c, :] for s in range(2)],
                                  [w[slot][DOWN][0:k, c, :] for w in (w_hi, w_lo)],
                                  start and c == 0, stop and c == KF - 1)
                ins.then_inc(down_done, 1)

            def fill_table(e, j, first):
                pe.wait_ge(vals_done, e + 1)
                if j == 0 and not first:
                    pe.wait_ge(tab_copied, (e - j) // 4 if isinstance(e, int) else tabs(e))
                W = NV * NBLK
                for t in range(NT):
                    ins = pe.matmul(bank[5][:, j * W:(j + 1) * W], S["onehot"][j % 2][:, t, :],
                                    S["vals"][j % 2][:, t, :, :].rearrange("p v a -> p (v a)"),
                                    start=t == 0, stop=t == NT - 1)
                ins.then_inc(tab_psum, 1)

            def fill_table_last(i):
                fill_table(4 * i + 3, 3, True)

            def pe_shared(i, first):
                nonlocal_i[0] = i
                for j in range(4):
                    g = 4 * i + j
                    half, t = j % 2, 2 * i + j // 2
                    gate_up(half, half, t, (j // 2) % 2)
                    if half:
                        par = (j // 2 + 1) % 2
                        turn_x(t + 1, par, i + 1 + (j // 2 + 1) // 2)
                        if not (first and j == 1):
                            pe.wait_ge(shared_added, t)
                        down(g - 1, 0, 0, True, False)
                    elif not (first and j == 0):
                        down(g - 1, 1, 1, False, True)
                    turn_h(g)
                    if j:
                        fill_table(g - 1, j - 1, first)
                    elif not first:
                        fill_table_last(i - 1)

            nonlocal_i = [0]

            def tabs(e):
                return nonlocal_i[0]

            turn_x(0, 0, 1)
            pe_shared(0, True)
            with pe.Fori(1, SH // 4) as i:
                pe_shared(i, False)
            fill_table_last(SH // 4 - 1)

            def pe_pair(i, first, last):
                for k in range(2 * MAIN):
                    r = 2 * MAIN * i + k
                    e, j = 2 * i + k // MAIN, k % MAIN
                    slot = (k // MAIN) % 2
                    gate_up(2 + e, slot, NT + r, k % 2)
                    if not (last and k == 2 * MAIN - 1):
                        turn_x(NT + r + 1, (k + 1) % 2, NT // 2 + MAIN * i + 1 + (k + 1) // 2)
                    if first and k == 0:
                        down(SH - 1, 1, 1, False, True)
                    else:
                        if first and k == 1:
                            pe.wait_ge(shared_added, NT)
                        elif k >= 1:
                            pe.wait_ge(y_scaled, r - 1)
                        else:
                            pe.wait_ge(y_scaled, r - 1)
                        down(SH + r - 1, 2 + e - (1 if j == 0 else 0), slot if j else 1 - slot, True, True)
                    turn_h(SH + r)
                if last:
                    r = 2 * MAIN * (i + 1)
                    pe.wait_ge(y_scaled, r - 1)
                    down(SH + r - 1, 2 + E - 1, 1, True, True)

            pe_pair(0, True, False)
            with pe.Fori(1, E // 2 - 1) as i:
                pe_pair(i, False, False)
            pe_pair(E // 2 - 1, False, True)

            main_added(pe)
            with pe.If(most_rows(pe) > MAIN * P):
                with pe.Fori(0, E) as e:
                    for j in range(REST):
                        q = REST * e + j
                        pe.wait_ge(o_x_in, 16 * (q + 1))
                        for c in range(KD):
                            ins = pe.transpose(bank[0][:, c * P:(c + 1) * P], o_x[:, c * P:(c + 1) * P], ident[:])
                        ins.then_inc(o_x_psum, 1)
                        pe.wait_ge(o_xT, q + 1)
                        pe.wait_ge(o_w_in, 64 * (e + 1))
                        for p in range(2):
                            for c in range(KD):
                                ins = pe.matmul(bank[1 + p][:, 0:F], o_xT_sb[:, c, :], raw[p][:, c, :],
                                                start=c == 0, stop=c == KD - 1)
                        ins.then_inc(o_gu, 1)
                        pe.wait_ge(o_h, q + 1)
                        for c in range(KF):
                            n = P if c < KF - 1 else FR
                            ins = pe.transpose(bank[3][0:n, c * P:(c + 1) * P], S["h"][:, c * P:c * P + n], ident[:])
                        ins.then_inc(o_h_psum, 1)
                        pe.wait_ge(o_hT, 2 * q + 2)
                        for c in range(KF):
                            n = P if c < KF - 1 else FR
                            ins = pe.matmul(bank[4][:], o_hT_sb[0:n, c, :], raw[DOWN][0:n, c, :],
                                            start=c == 0, stop=c == KF - 1)
                        ins.then_inc(o_down, 1)
                pe.wait_ge(o_down, REST * E)


_INS = ['x', 'ctx_1024', 'g_xattn', 'g_ffn', 'L0_xattn_Wq', 'L0_xattn_bq', 'L0_xattn_Wk', 'L0_xattn_bk',
        'L0_ffn_wg_router', 'L0_ffn_w_gate', 'L0_ffn_w_up', 'L0_ffn_w_down', 'L0_ffn_ws_gate', 'L0_ffn_ws_up',
        'L0_ffn_ws_down']
_OUT = ((4, 512, 512), 'float32')


def kernel(**inputs):
    import numpy as _np
    import concourse.bacc as _bacc
    from concourse import mybir as _mybir
    from concourse.bass_utils import run_bass_kernel_spmd as _run

    nc = _bacc.Bacc("TRN2", target_bir_lowering=False, num_devices=1)
    arrays, args = {}, []
    for name in _INS:
        a = _np.ascontiguousarray(inputs[name])
        arrays[f"in_{name}"] = a
        args.append(nc.dram_tensor(f"in_{name}", a.shape, _mybir.dt.from_np(a.dtype), kind="ExternalInput").ap())
    shape, dtype = _OUT
    out = nc.dram_tensor("out_0", shape, _mybir.dt.from_np(_np.dtype(dtype)), kind="ExternalOutput").ap()
    gated_attention_moe(nc, *args, out)
    r = _run(nc, [arrays], core_ids=[0])
    return r.results[0]["out_0"]
```
